# Optimizing a Trainium2 kernel written in Bass

```python
import numpy as np
import jax
import jax.numpy as jnp

def _softmax(x, axis=-1):
    return jax.nn.softmax(x, axis=axis)

def _gelu(x):
    return jax.nn.gelu(x, approximate=True)

def _silu(x):
    return jax.nn.silu(x)

def _sigmoid(x):
    return jax.nn.sigmoid(x)

def _layernorm(x, axis=-1, eps=1e-05):
    m = jnp.mean(x, axis=axis, keepdims=True)
    v = jnp.var(x, axis=axis, keepdims=True)
    return (x - m) / jnp.sqrt(v + eps)

def _scatter_add(tgt, idx, src, axis=0):
    return tgt.at[idx].add(src)

def _segment_sum(src, seg, n):
    return jax.ops.segment_sum(src, seg, n)
kernel_name = 'mk_sandwich_d1_jaxref_r4_669de5'

def setup_inputs(seed: int=0):
    np.random.seed(seed)
    _w = jnp.asarray

    def _L0_attn_setup():
        import jax, jax.numpy as jnp
        import numpy as np
        NUM_HEADS = 16
        key = jax.random.key(seed)
        ks = jax.random.split(key, 5)
        B, N, C = (4, 512, 256)
        s = 0.02
        return {'x': jax.random.normal(ks[0], (B, N, C), jnp.float32), 'w_qkv': jax.random.normal(ks[1], (C, 3 * C), jnp.float32) * s, 'b_qkv': jnp.zeros((3 * C,), jnp.float32), 'w_proj': jax.random.normal(ks[2], (C, C), jnp.float32) * s, 'b_proj': jnp.zeros((C,), jnp.float32)}
    _L0_attn_in = _L0_attn_setup()

    def _L0_ffn_setup():
        import math
        import jax, jax.numpy as jnp
        import numpy as np
        B, S, H, BOT, RD, N, K = (4, 512, 256, 128, 48, 1024, 8)
        key = jax.random.key(seed)
        ks = jax.random.split(key, 12)
        hidden_states = jax.random.normal(ks[0], (B, S, H), jnp.float32)
        q_proj_w = jax.random.normal(ks[1], (BOT, H), jnp.float32) * (1.0 / math.sqrt(H))
        router_w = jax.random.normal(ks[2], (RD, BOT), jnp.float32) * (1.0 / math.sqrt(BOT))
        aux_keys = jax.random.normal(ks[3], (N, BOT), jnp.float32) * 0.01
        aux_values = jax.random.normal(ks[4], (N, H), jnp.float32) * 0.02
        reliability_mask = jax.random.uniform(ks[5], (N,), jnp.float32)
        unc_w1 = jax.random.normal(ks[6], (H // 4, H), jnp.float32) * (1.0 / math.sqrt(H))
        unc_b1 = jnp.zeros((H // 4,), jnp.float32)
        unc_w2 = jax.random.normal(ks[7], (1, H // 4), jnp.float32) * 0.02
        unc_b2 = jnp.zeros((1,), jnp.float32)
        gate_w1 = jnp.asarray(0.5, jnp.float32)
        gate_bias = jnp.asarray(-1.0, jnp.float32)
        return {'hidden_states': hidden_states, 'q_proj_w': q_proj_w, 'router_w': router_w, 'aux_keys': aux_keys, 'aux_values': aux_values, 'reliability_mask': reliability_mask, 'unc_w1': unc_w1, 'unc_b1': unc_b1, 'unc_w2': unc_w2, 'unc_b2': unc_b2, 'gate_w1': gate_w1, 'gate_bias': gate_bias}
    _L0_ffn_in = _L0_ffn_setup()
    _d = {'L0_attn_x': _L0_attn_in['x'], 'L0_attn_w_qkv': _L0_attn_in['w_qkv'], 'L0_attn_b_qkv': _L0_attn_in['b_qkv'], 'L0_attn_w_proj': _L0_attn_in['w_proj'], 'L0_attn_b_proj': _L0_attn_in['b_proj'], 'L0_ffn_q_proj_w': _L0_ffn_in['q_proj_w'], 'L0_ffn_router_w': _L0_ffn_in['router_w'], 'L0_ffn_aux_keys': _L0_ffn_in['aux_keys'], 'L0_ffn_aux_values': _L0_ffn_in['aux_values'], 'L0_ffn_reliability_mask': _L0_ffn_in['reliability_mask'], 'L0_ffn_unc_w1': _L0_ffn_in['unc_w1'], 'L0_ffn_unc_b1': _L0_ffn_in['unc_b1'], 'L0_ffn_unc_w2': _L0_ffn_in['unc_w2'], 'L0_ffn_unc_b2': _L0_ffn_in['unc_b2'], 'L0_ffn_gate_w1': _L0_ffn_in['gate_w1'], 'L0_ffn_gate_bias': _L0_ffn_in['gate_bias']}
    _x0 = _d['L0_attn_x']
    _d['L0_attn_x'] = jax.random.normal(jax.random.fold_in(jax.random.key(seed), 1), (1, 4096, 256), dtype=_x0.dtype)
    del _x0
    return _d

def reference(L0_attn_x, L0_attn_w_qkv, L0_attn_b_qkv, L0_attn_w_proj, L0_attn_b_proj, L0_ffn_q_proj_w, L0_ffn_router_w, L0_ffn_aux_keys, L0_ffn_aux_values, L0_ffn_reliability_mask, L0_ffn_unc_w1, L0_ffn_unc_b1, L0_ffn_unc_w2, L0_ffn_unc_b2, L0_ffn_gate_w1, L0_ffn_gate_bias):

    def _L0_attn_ref(x, w_qkv, b_qkv, w_proj, b_proj):
        import jax, jax.numpy as jnp
        import numpy as np
        NUM_HEADS = 16
        B, N, C = x.shape
        H = NUM_HEADS
        D = C // H
        scale = D ** (-0.5)
        qkv = x @ w_qkv + b_qkv
        qkv = qkv.reshape(B, N, 3, H, D)
        q, k, v = (jnp.moveaxis(qkv, 2, 0)[i] for i in range(3))
        scores = jnp.einsum('bqhd,bkhd->bhqk', q.astype(jnp.float32), k.astype(jnp.float32)) * scale
        attn = jax.nn.softmax(scores, axis=-1).astype(q.dtype)
        out = jnp.einsum('bhqk,bkhd->bqhd', attn, v).reshape(B, N, C)
        return out @ w_proj + b_proj

    def _L0_ffn_ref(hidden_states, q_proj_w, router_w, aux_keys, aux_values, reliability_mask, unc_w1, unc_b1, unc_w2, unc_b2, gate_w1, gate_bias):
        import math
        import jax, jax.numpy as jnp
        import numpy as np
        B, S, H, BOT, RD, N, K = (4, 512, 256, 128, 48, 1024, 8)
        query = jnp.einsum('bsh,dh->bsd', hidden_states, q_proj_w)
        rq = jnp.einsum('bsd,rd->bsr', query, router_w)
        rk = jnp.einsum('nd,rd->nr', aux_keys, router_w)
        scores = jnp.einsum('bsr,nr->bsn', rq, rk) / math.sqrt(RD)
        scores = scores + reliability_mask[None, None, :]
        top_scores, top_idx = jax.lax.top_k(scores, K)
        mean = hidden_states.mean(axis=-1, keepdims=True)
        variance = ((hidden_states - mean) ** 2).mean(axis=-1)
        log_var = jnp.log1p(variance)
        normalized_var = log_var / (log_var.mean() + 1e-06)
        h1 = jax.nn.gelu(jnp.einsum('bsh,fh->bsf', hidden_states, unc_w1) + unc_b1, approximate=False)
        learned = (jnp.einsum('bsf,of->bso', h1, unc_w2) + unc_b2)[..., 0]
        uncertainty = jnp.clip(normalized_var * 0.5 + jax.nn.sigmoid(learned) * 2.5, 0.0, 5.0)
        gate = jax.nn.sigmoid(gate_w1 * uncertainty + gate_bias)
        w = jax.nn.softmax(top_scores, axis=-1)
        v = aux_values[top_idx]
        agg = jnp.einsum('bsk,bskh->bsh', w, v)
        out = hidden_states + gate[..., None] * agg
        return out
    x = L0_attn_x
    x = x + _layernorm(_L0_attn_ref(_layernorm(x, axis=-1), L0_attn_w_qkv, L0_attn_b_qkv, L0_attn_w_proj, L0_attn_b_proj), axis=-1)
    x = x + _layernorm(_L0_ffn_ref(_layernorm(x, axis=-1), L0_ffn_q_proj_w, L0_ffn_router_w, L0_ffn_aux_keys, L0_ffn_aux_values, L0_ffn_reliability_mask, L0_ffn_unc_w1, L0_ffn_unc_b1, L0_ffn_unc_w2, L0_ffn_unc_b2, L0_ffn_gate_w1, L0_ffn_gate_bias), axis=-1)
    return x

_drawn_inputs = setup_inputs


def setup_inputs(seed=0):
    import zlib

    import numpy as np

    out = dict(_drawn_inputs(seed))
    spreads = {'L0_attn_b_qkv': (0.0, 0.1), 'L0_attn_b_proj': (0.0, 0.1), 'L0_ffn_unc_b1': (0.0, 0.8)}
    factors = {'L0_attn_w_qkv': 5.034,
     'L0_ffn_q_proj_w': 8.0,
     'L0_ffn_router_w': 8.0,
     'L0_ffn_aux_keys': 8.0,
     'L0_ffn_aux_values': 8.0,
     'L0_ffn_unc_w1': 8.0,
     'L0_ffn_unc_w2': 8.0}
    for name, (base, spread) in spreads.items():
        noise = np.random.default_rng([zlib.crc32(name.encode()), seed]).standard_normal(out[name].shape)
        drawn = base * np.exp(spread * noise) if base else spread * noise
        out[name] = jnp.asarray(drawn.astype(out[name].dtype))
    for name, factor in factors.items():
        out[name] = (out[name] * factor).astype(out[name].dtype)
    return out
```

```python
from contextlib import ExitStack

import concourse.bass as bass
from concourse import mybir

F32 = mybir.dt.float32
BF16 = mybir.dt.bfloat16
ALU = mybir.AluOpType
ACT = mybir.ActivationFunctionType
AX = mybir.AxisListType

P = 128
CH = 512
EPS = 1e-5
NB = 3
SLOT_Q = [0, 0, 1, 0, 1, 2]
SLOT_K = [0, 1, 0, 2, 1, 0]
TAKEN = -3.0e38


def sandwich_kernel(nc, x, w_qkv, b_qkv, w_proj, b_proj, q_proj_w, router_w, aux_keys, aux_values,
                    reliability_mask, unc_w1, unc_b1, unc_w2, unc_b2, gate_w1, gate_bias, out):
    _, T, C = x.shape
    H = 16
    D = C // H
    NT = T // P
    NC = T // CH
    TPC = CH // P
    CC = C // P
    BOT = q_proj_w.shape[0]
    RD = router_w.shape[0]
    N = aux_keys.shape[0]
    NV = N // P
    F1 = unc_w1.shape[0]
    SCALE = float(D) ** -0.5
    RSQ = float(RD) ** -0.5
    ROWS = 6 * D
    MROWS = 3
    KG = NT // 4
    PADQ = (NC + 1) * CH
    ITS = H * NC
    MASKROW = 64
    assert ROWS == 96 and C == 256 and T == 4096 and BOT == P and RD <= MASKROW and N == 1024

    x_t = x[0].rearrange("(t p) c -> p t c", p=P)
    out_t = out[0].rearrange("(t p) c -> p t c", p=P)
    parts_dram = nc.dram_tensor("qk_parts", (2, 3, C, T), BF16, kind="Internal").ap()

    with ExitStack() as ctx:
        def sb(name, shape, dt=F32):
            return ctx.enter_context(nc.sbuf_tensor(name, shape, dt))

        def sem(name):
            return ctx.enter_context(nc.semaphore(name))

        ps = ctx.enter_context(nc.psum_tensor("ps", [P, 8, CH], F32))

        x_sb = sb("x_sb", [P, NT, C])
        v_all = sb("v_all", [P, NT * C])
        attn = sb("attn", [P, NC * TPC * C + 4 * D])
        work = sb("work", [P, 8192])
        q_raw = sb("q_raw", [P, NB * PADQ // 2])
        k_raw = sb("k_raw", [P, NB * T // 2])
        v_head = sb("v_head", [P, NB, NT, 32])
        o_sb = sb("o_sb", [P, CH])
        ident = sb("ident", [P, P])
        ident_bf = sb("ident_bf", [P, P], BF16)
        sel = sb("sel", [P, D + 1])
        stats = sb("stats", [P, NT, 6])
        mv = sb("mv", [P, NT, 2])
        rstd = sb("rstd", [P, NT])
        veps = sb("veps", [P, NT])
        hvar = sb("hvar", [P, NT])
        minus_half = sb("minus_half", [P, NT])
        partial = sb("partial", [P, TPC, 4])
        negmax = sb("negmax", [P, TPC])
        nm_rest = sb("nm_rest", [P, 2, TPC])
        nm_parts = sb("nm_parts", [P, TPC, MROWS], BF16)
        nm_all = sb("nm_all", [P, NB, (NC + 1) * TPC, MROWS], BF16)
        rinv = sb("rinv", [P, TPC])

        q_stack = q_raw[:, :].bitcast(BF16).rearrange("p (b t) -> p b t", b=NB)
        k_stack = k_raw[:, :].bitcast(BF16).rearrange("p (b t) -> p b t", b=NB)
        v_rows = v_all[:, :].rearrange("p (t c) -> p t c", c=C)

        xn = work[:, 0:1024].rearrange("p (t c) -> p t c", t=TPC)
        xnT = work[:, 1024:2048].rearrange("p (k t) -> p k t", k=CC)
        wqkv = work[:, 2048:3584].rearrange("p (k n) -> p k n", k=CC)
        qk_f32 = work[:, 3584:4608].rearrange("p (b t) -> p b t", b=2)
        qk_rest = work[:, 4608:5632].rearrange("p (b t) -> p b t", b=2)
        qk_part = work[:, 5632:7168].bitcast(BF16).rearrange("p (b r t) -> p b r t", b=2, r=3)
        bv = work[:, 7168:7680].rearrange("p (a c) -> p a c", a=2)
        bqk = work[:, 7680:7684]
        probs = work[:, :].rearrange("p (r j t) -> p r j t", r=4, j=4)
        stage = work[:, 0:1024].rearrange("p (t c) -> p t c", t=TPC)
        aT = work[:, 1024:2048].rearrange("p (k t) -> p k t", k=CC)
        y = work[:, 2048:3072].rearrange("p (t c) -> p t c", t=TPC)
        hT = work[:, 3072:4096].rearrange("p (k t) -> p k t", k=CC)
        queryT = work[:, 4096:4608]
        rqT = work[:, 4608:5120]
        g1T = work[:, 5120:5632]
        picked_flat = [work[:, 5632:6656], work[:, 1024:2048]]
        wts_flat = [work[:, 6656:7680], work[:, 2048:3072]]
        picked = [v.rearrange("p (a n) -> p a n", a=2) for v in picked_flat]
        wts = [v.rearrange("p (a n) -> p a n", a=2) for v in wts_flat]
        sc_bank = [4, 0]
        o2 = work[:, 0:1024].rearrange("p (t c) -> p t c", t=TPC)
        res = [work[:, 1024 * (b + 1):1024 * (b + 2)].rearrange("p (t c) -> p t c", t=TPC) for b in range(2)]
        wproj = k_raw[:, 0:512].rearrange("p (k n) -> p k n", k=CC)
        bproj = k_raw[:, 512:1024].rearrange("p (a c) -> p a c", a=2)
        values = k_raw[:, 1024:3072].rearrange("p (v c) -> p v c", v=NV)
        keys = k_raw[:, 3072:4096].rearrange("p (v c) -> p v c", v=NV)
        keysT = k_raw[:, 4096:5120]
        rkT = k_raw[:, 5120:6144]
        qpw = q_raw[:, 0:256]
        qpT = q_raw[:, 256:512].rearrange("p (k n) -> p k n", k=CC)
        routw = q_raw[:, 512:640]
        routT = q_raw[:, 640:640 + RD]
        u1w = q_raw[:, 704:960]
        u1T = q_raw[:, 960:1088].rearrange("p (k n) -> p k n", k=CC)
        small = q_raw[:, 1088:1152]
        u1b, u2w, u2b, gw, gb = (small[:, i:i + 1] for i in range(5))
        lvs, lvm, lvr = (small[:, i:i + 1] for i in range(5, 8))
        ones = q_raw[:, 1152:1280]
        top8 = q_raw[:, 1440:1472].rearrange("p (i e) -> p i e", i=TPC)
        nbias = q_raw[:, 1280:1284]
        wsum = q_raw[:, 1284:1288]
        wrec = q_raw[:, 1288:1292]
        lv = q_raw[:, 1312:1344]
        learned = q_raw[:, 1344:1376]
        gate = q_raw[:, 1376:1408]
        gtmp = q_raw[:, 1408:1440]
        wT = q_raw[:, 1536:2560].rearrange("p (v t) -> p v t", v=NV)
        wT2 = q_raw[:, 1536:2560].rearrange("p (a n) -> p a n", a=2)

        attn_h = attn[:, 4 * D:].rearrange("p (h t d) -> p h t d", h=H, t=NT)
        agg = attn[:, 4 * D:].rearrange("p (t c) -> p t c", c=C)

        x_in = [sem(f"x_in{c}") for c in range(NC)]
        w_in = sem("w_in")
        primed = sem("primed")
        consts = sem("consts")
        st_done = sem("st_done")
        rstd_done = sem("rstd_done")
        pool_own = sem("pool_own")
        xn_ready = sem("xn_ready")
        t_ready = sem("t_ready")
        xnT_ready = sem("xnT_ready")
        qk_ready = sem("qk_ready")
        f_ready = sem("f_ready")
        split_own = sem("split_own")
        split_done = sem("split_done")
        parts_out = [sem("parts_out0"), sem("parts_out1")]
        v_ready = sem("v_ready")
        v_evac = sem("v_evac")
        stack_in = [sem(f"stack_in{b}") for b in range(NB)]
        s_ready = sem("s_ready")
        exp_done = sem("exp_done")
        m_ready = sem("m_ready")
        max_used = sem("max_used")
        negmax_ready = sem("negmax_ready")
        nmparts_ready = sem("nmparts_ready")
        vhead_ready = sem("vhead_ready")
        pv_done = sem("pv_done")
        o_evac = sem("o_evac")
        comb_ready = sem("comb_ready")
        rinv_done = sem("rinv_done")
        comb_used = sem("comb_used")
        mrow_ready = sem("mrow_ready")
        mrow_done = sem("mrow_done")
        dve_passed = sem("dve_passed")
        pool_passed = sem("pool_passed")
        w3_in = sem("w3_in")
        w3_init = sem("w3_init")
        w3_t = sem("w3_t")
        w3_e = sem("w3_e")
        pow_own = sem("pow_own")
        stage_ready = sem("stage_ready")
        aT_psum = sem("aT_psum")
        aT_ready = sem("aT_ready")
        y_psum = sem("y_psum")
        y_own = sem("y_own")
        y_evac = sem("y_evac")
        var_ready = sem("var_ready")
        rs_ready = sem("rs_ready")
        h_ready = sem("h_ready")
        hT_psum = sem("hT_psum")
        hT_ready = sem("hT_ready")
        qy_psum = sem("qy_psum")
        qy_ready = sem("qy_ready")
        rq_psum = sem("rq_psum")
        rq_ready = sem("rq_ready")
        u_psum = sem("u_psum")
        u_ready = sem("u_ready")
        l_psum = sem("l_psum")
        l_ready = sem("l_ready")
        sc_psum = sem("sc_psum")
        top_ready = sem("top_ready")
        nb_ready = sem("nb_ready")
        picked_ready = sem("picked_ready")
        e_ready = sem("e_ready")
        w_sum = sem("w_sum")
        wr_ready = sem("wr_ready")
        wT_psum = sem("wT_psum")
        wT_ready = sem("wT_ready")
        agg_psum = sem("agg_psum")
        agg_ready = sem("agg_ready")
        lv_ready = sem("lv_ready")
        lv_own = sem("lv_own")
        lvt_ready = sem("lvt_ready")
        g_own = sem("g_own")
        g_e = sem("g_e")
        g_a = sem("g_a")
        o_own = sem("o_own")
        o_var = sem("o_var")
        o_rs = sem("o_rs")
        res_ready = sem("res_ready")
        out_done = [sem("out_done0"), sem("out_done1")]

        CREDIT = {exp_done: 2, max_used: 2, pv_done: 4, o_evac: 1, comb_used: 1, nmparts_ready: 1, negmax_ready: 1, res_ready: 1,
                  f_ready: 4, split_done: 2, v_evac: 2, aT_psum: 1, hT_psum: 1, y_evac: 2, e_ready: 2, wT_ready: 1,
                  agg_ready: 2, l_ready: 1, agg_psum: 1,
                  wT_psum: 2}

        block = ctx.enter_context(nc.Block())

        @block.sync
        def _(sp):
            for c in range(NC):
                sp.dma_start(x_sb[:, TPC * c:TPC * (c + 1), :], x_t[:, TPC * c:TPC * (c + 1), :]).then_inc(x_in[c], 16)
            with sp.Fori(0, NC) as c:
                for g in range(4):
                    sp.wait_ge(split_done, c * 4 + (g + 1 + CREDIT[split_done]))
                    dst = parts_dram[g // 2, :, (g % 2) * P:(g % 2 + 1) * P, bass.ds(c * CH, CH)]
                    sp.dma_start(dst.rearrange("r f t -> f r t"), qk_part[:, g % 2, :, :]).then_inc(parts_out[g % 2], 16)
            for b in range(2):
                sp.wait_ge(parts_out[b], 16 * (2 * NC + 1))

            def load_stack(h, b):
                for s in range(6):
                    for stack, qk, part in ((k_stack, 1, SLOT_K[s]), (q_stack, 0, SLOT_Q[s])):
                        sp.dma_start(stack[D * s:D * (s + 1), b, 0:T], parts_dram[qk, part, bass.ds(h * D, D), :]
                                     ).then_inc(stack_in[b], 16)

            for b in range(NB):
                load_stack(b, b)
            with sp.Fori(1, H // NB) as r:
                for b in range(NB):
                    sp.wait_ge(pv_done, r * (NB * NC * KG) + ((b - 2) * NC * KG + CREDIT[pv_done]))
                    load_stack(r * NB + b, b)
            sp.wait_ge(pv_done, (H - 3) * NC * KG + CREDIT[pv_done])
            load_stack(H - 1, (H - 1) % NB)

            sp.wait_ge(pv_done, ITS * KG + CREDIT[pv_done])
            sp.wait_ge(w3_init, 3)
            for dst, src in (
                (wproj, w_proj.rearrange("(k p) n -> p k n", p=P)),
                (bproj[:, 0, :], b_proj.partition_broadcast(P)),
                (bproj[:, 1, :], b_proj.partition_broadcast(P)),
                (keys, aux_keys.rearrange("(v p) d -> p v d", p=P)),
                (qpw, q_proj_w),
                (routw[0:RD, :], router_w),
                (u1w[0:F1, :], unc_w1),
                (u1b[0:F1, :], unc_b1.rearrange("(f a) -> f a", a=1)),
                (u2w[0:F1, :], unc_w2.rearrange("a f -> f a")),
                (u2b, unc_b2.partition_broadcast(P)),
                (gw, gate_w1.partition_broadcast(P)),
                (gb, gate_bias.partition_broadcast(P)),
                (rkT[MASKROW:MASKROW + 1, :], reliability_mask.rearrange("(a n) -> a n", a=1)),
                (values, aux_values.rearrange("(v p) d -> p v d", p=P)),
            ):
                sp.dma_start(dst, src, allow_slow_non_contiguous=True).then_inc(w3_in, 16)

            with sp.Fori(0, NC // 2) as c2:
                for b in range(2):
                    sp.wait_ge(res_ready, c2 * 2 + (b + 1 + CREDIT[res_ready]))
                    sp.dma_start(out_t[:, bass.ds(c2 * (2 * TPC) + b * TPC, TPC), :], res[b]).then_inc(out_done[b], 16)
            for b in range(2):
                sp.wait_ge(out_done[b], 16 * (NC // 2 + 1))

        W3_LOADS = 14

        @block.gpsimd
        def _(pool):
            pool.dma_start(wqkv, w_qkv.rearrange("(k p) n -> p k n", p=P)).then_inc(w_in, 16)
            pool.dma_start(bqk, b_qkv[0:2 * C].rearrange("(g p) -> p g", p=P), allow_slow_non_contiguous=True).then_inc(w_in, 16)
            for a in range(2):
                pool.dma_start(bv[:, a, :], b_qkv[2 * C:3 * C].partition_broadcast(P)).then_inc(w_in, 16)
            pool.memset(minus_half[:], -0.5).then_inc(consts, 1)
            pool.memset(ident[:], 0.0).then_inc(consts, 1)
            pool.memset(sel[:], 0.0).then_inc(consts, 1)
            pool.memset(o_sb[:], 1.0).then_inc(consts, 1)
            pool.memset(nm_all[:], 0.0).then_inc(consts, 1)
            pool.wait_ge(consts, 5)
            pool.memset(k_stack[ROWS:ROWS + MROWS, :, :], 1.0).then_inc(consts, 1)
            pool.wait_ge(consts, 6)
            pool.memset(v_head[:], 0.0).then_inc(consts, 1)
            pool.wait_ge(consts, 7)
            pool.affine_select(out=ident[:], in_=ident[:], compare_op=ALU.not_equal, fill=1.0, base=0,
                               pattern=[[-1, P]], channel_multiplier=1).then_inc(consts, 1)
            pool.memset(v_head[:, :, :, D], 1.0).then_inc(consts, 1)
            pool.wait_ge(consts, 9)
            for j in range(4):
                pool.affine_select(out=sel[:], in_=sel[:], compare_op=ALU.not_equal, fill=1.0, base=-32 * j,
                                   pattern=[[-1, D + 1]], channel_multiplier=1).then_inc(consts, 1)
                pool.wait_ge(consts, 10 + j)
            pool.tensor_copy(ident_bf[:], ident[:]).then_inc(consts, 1)
            pool.wait_ge(consts, 14)
            for s, n in CREDIT.items():
                if n:
                    pool.sem_inc(s, n)
            for s in parts_out + out_done:
                pool.sem_inc(s, 16)
            pool.sem_inc(primed, 1)

            pool.wait_ge(st_done, 2 * NT)
            pool.tensor_scalar(veps[:, :], mv[:, :, 1], EPS, None, ALU.add).then_inc(pool_own, 1)
            pool.wait_ge(pool_own, 1)
            pool.tensor_tensor(rstd[:, :], veps[:, :], minus_half[:, :], ALU.pow).then_inc(rstd_done, 1)

            def copy_v(h, b):
                pool.tensor_copy(v_head[:, b, :, 0:D], v_rows[:, :, bass.ds(h * D, D)]).then_inc(vhead_ready, 1)

            pool.wait_ge(v_evac, 2 * NC + CREDIT[v_evac])
            copy_v(0, 0)

            def split_max(mi, b1, c):
                pool.wait_ge(negmax_ready, mi + 1 + CREDIT[negmax_ready])
                pool.sem_inc(pool_passed, 1)
                pool.tensor_copy(nm_parts[:, :, 0], negmax[:, :]).then_inc(pool_own, 1)
                pool.wait_ge(pool_own, mi * 5 + 2)
                pool.tensor_tensor(nm_rest[:, 0, :], negmax[:, :], nm_parts[:, :, 0], ALU.subtract).then_inc(pool_own, 1)
                pool.wait_ge(pool_own, mi * 5 + 3)
                pool.sem_inc(pool_passed, 1)
                pool.tensor_copy(nm_parts[:, :, 1], nm_rest[:, 0, :]).then_inc(pool_own, 1)
                pool.wait_ge(pool_own, mi * 5 + 4)
                pool.tensor_tensor(nm_rest[:, 1, :], nm_rest[:, 0, :], nm_parts[:, :, 1], ALU.subtract).then_inc(pool_own, 1)
                pool.wait_ge(pool_own, mi * 5 + 5)
                pool.sem_inc(pool_passed, 1)
                pool.tensor_copy(nm_parts[:, :, 2], nm_rest[:, 1, :]).then_inc(pool_own, 1)
                pool.wait_ge(pool_own, mi * 5 + 6)
                pool.sem_inc(pool_passed, 1)
                pool.tensor_copy(nm_all[:, b1, bass.ds(c * TPC, TPC), :], nm_parts[:, :, :]).then_inc(nmparts_ready, 1)

            with pool.Fori(0, NC) as c:
                split_max(c, 0, c)
            with pool.Fori(0, H // NB) as r:
                for b in range(NB):
                    pool.wait_ge(pv_done, r * (NB * NC * KG) + (b * NC * KG + CREDIT[pv_done]))
                    pool.sem_inc(pool_passed, 1)
                    copy_v(r * NB + (b + 1), (b + 1) % NB)
                    with pool.Fori(0, NC) as c:
                        split_max(r * (NB * NC) + c + (b + 1) * NC, (b + 1) % NB, c)

            pool.wait_ge(pv_done, ITS * KG + CREDIT[pv_done])
            pool.memset(rkT, 0.0).then_inc(w3_init, 1)
            pool.memset(ones, 1.0).then_inc(w3_init, 1)
            pool.memset(rqT, 0.0).then_inc(w3_init, 1)
            pool.wait_ge(w3_init, 3)
            pool.memset(rqT[MASKROW:MASKROW + 1, :], 1.0).then_inc(w3_init, 1)
            pool.wait_ge(w3_init, 4)

            def powers(n, have_var, rs):
                pool.sem_inc(pool_passed, 1)
                pool.tensor_scalar(veps[:, 0:TPC], mv[:, 0:TPC, 1], EPS, None, ALU.add).then_inc(pow_own, 1)
                pool.wait_ge(pow_own, n)
                pool.tensor_tensor(rstd[:, 0:TPC], veps[:, 0:TPC], minus_half[:, 0:TPC], ALU.pow).then_inc(rs, 1)

            pool.wait_ge(comb_used, ITS + 1 + CREDIT[comb_used])
            with pool.Fori(0, NC) as c:
                pool.wait_ge(aT_psum, c + CREDIT[aT_psum])
                pool.sem_inc(pool_passed, 1)
                for i in range(TPC):
                    last = pool.tensor_copy(stage[:, i, :].rearrange("p (h d) -> p h d", h=H),
                                            attn_h[:, :, bass.ds(c * TPC + i, 1), :].rearrange("p h a d -> p (h a) d"))
                last.then_inc(stage_ready, 1)
                for k in range(2):
                    pool.wait_ge(var_ready, c * 2 + (k + 1))
                    powers(c * 2 + (k + 1), var_ready, rs_ready)
            pool.wait_ge(h_ready, NC)
            with pool.Fori(0, NC) as c:
                pool.wait_ge(hT_psum, c + CREDIT[hT_psum])
                pool.sem_inc(pool_passed, 1)
                pool.tensor_copy(stage, v_rows[:, bass.ds(c * TPC, TPC), :]).then_inc(stage_ready, 1)
            with pool.Fori(0, NC) as c:
                pool.wait_ge(o_var, c + 1)
                powers(c + (2 * NC + 1), o_var, o_rs)

        @block.scalar
        def _(act):
            act.wait_ge(w_in, 64)

            def move_xnT(c):
                act.wait_ge(t_ready, c + 1)
                act.activation(xnT, ps[:, 0:2, :], ACT.Copy).then_inc(xnT_ready, 1)

            def evacuate_qk(c):
                for g in range(4):
                    act.wait_ge(qk_ready, c * 4 + (g + 1))
                    act.wait_ge(split_done, c * 4 + (g + 1))
                    act.wait_ge(parts_out[g % 2], c * 32 + 16 * (g // 2 + 1))
                    act.activation(qk_f32[:, g % 2, :], ps[:, 2 + g % 2, :], ACT.Identity,
                                   bias=bqk[:, g:g + 1]).then_inc(f_ready, 1)
                    act.activation(qk_part[:, g % 2, 0, :], ps[:, 2 + g % 2, :], ACT.Identity,
                                   bias=bqk[:, g:g + 1]).then_inc(f_ready, 1)

            move_xnT(0)
            with act.Fori(0, NC - 1) as c:
                evacuate_qk(c)
                act.wait_ge(v_ready, c * 2 + 2)
                move_xnT(c + 1)
            evacuate_qk(NC - 1)

            def move_max_row(b, c, n):
                act.wait_ge(mrow_ready, n)
                act.activation(q_stack[ROWS:ROWS + MROWS, b, bass.ds(c * CH, CH)], ps[0:MROWS, 7, :],
                               ACT.Copy).then_inc(mrow_done, 1)

            def attend(it, b, c, rows):
                for g in range(KG):
                    act.wait_ge(pv_done, it * KG + (g + 1))
                    for i in range(4):
                        act.wait_ge(s_ready, it * NT + (4 * g + i + 1))
                        act.activation(probs[:, g % 4, i, :], ps[:, 4 + i % 2, :], ACT.Exp,
                                       scale=SCALE).then_inc(exp_done, 1)
                    if g == 4:
                        move_max_row(b, c + 1, rows + c + 2)
                act.wait_ge(pv_done, it * KG + (KG + CREDIT[pv_done]))
                act.wait_ge(comb_ready, it + 1)
                act.activation(o_sb[:, :], ps[:, 6, :], ACT.Copy).then_inc(o_evac, 1)

            with act.Fori(0, H // NB) as r:
                for b in range(NB):
                    rows = r * (NB * (NC + 1)) + b * (NC + 1)
                    move_max_row(b, 0, rows + 1)
                    with act.Fori(0, NC) as c:
                        attend(r * (NB * NC) + c + b * NC, b, c, rows)
            rows = (H - 1) * (NC + 1)
            move_max_row(0, 0, rows + 1)
            with act.Fori(0, NC) as c:
                attend(c + (H - 1) * NC, 0, c, rows)

            with act.Fori(0, NC) as c:
                act.wait_ge(aT_psum, c + 1 + CREDIT[aT_psum])
                act.activation(aT, ps[:, 0:2, :], ACT.Copy).then_inc(aT_ready, 1)
            with act.Fori(0, NC) as c:
                act.wait_ge(hT_psum, c + 1 + CREDIT[hT_psum])
                act.activation(hT, ps[:, 0:2, :], ACT.Copy).then_inc(hT_ready, 1)
                act.wait_ge(u_psum, c + 1)
                act.activation(g1T[0:F1, :], ps[0:F1, 3, :], ACT.Gelu, bias=u1b[0:F1, :]).then_inc(u_ready, 1)
                act.wait_ge(qy_psum, c + 1)
                act.activation(queryT, ps[:, 2, :], ACT.Copy).then_inc(qy_ready, 1)
                act.wait_ge(rq_psum, c + 1)
                act.activation(rqT[0:RD, :], ps[0:RD, 3, :], ACT.Copy).then_inc(rq_ready, 1)
                for i in range(TPC):
                    n = c * TPC + i
                    act.wait_ge(picked_ready, n + 1)
                    act.wait_ge(wT_psum, n - 1 + CREDIT[wT_psum])
                    act.activation(wts[i % 2], ps[:, sc_bank[i % 2]:sc_bank[i % 2] + 2, :], ACT.Exp,
                                   bias=nbias[:, i:i + 1], scale=RSQ).then_inc(e_ready, 1)
                    act.wait_ge(wT_psum, n + 1 + CREDIT[wT_psum])
                    act.wait_ge(agg_psum, n + CREDIT[agg_psum])
                    act.activation(wT2, ps[:, 6:8, :], ACT.Copy).then_inc(wT_ready, 1)
            act.activation(lv, hvar[:, :], ACT.Ln, bias=1.0).then_inc(lv_ready, 1)
            act.wait_ge(g_own, 3)
            act.activation(gtmp, learned, ACT.Exp, scale=-1.0).then_inc(g_e, 1)
            act.wait_ge(g_a, 1)
            act.activation(gtmp, gate, ACT.Exp, scale=-1.0).then_inc(g_e, 1)

        @block.vector
        def _(dve):
            for c in range(NC):
                dve.wait_ge(x_in[c], 16)
                for i in range(TPC):
                    dve.bn_stats(stats[:, c * TPC + i, :], x_sb[:, c * TPC + i, :]).then_inc(st_done, 1)
            dve.wait_ge(st_done, NT)
            for t in range(NT):
                dve.bn_aggr(mv[:, t, :], stats[:, t, :]).then_inc(st_done, 1)
            dve.wait_ge(rstd_done, 1)
            dve.wait_ge(w_in, 64)
            dve.wait_ge(primed, 1)

            def norm_chunk(c):
                for i in range(TPC):
                    t = c * TPC + i
                    dve.tensor_scalar(xn[:, i, :], x_sb[:, bass.ds(t, 1), :].rearrange("p a c -> p (a c)"),
                                      mv[:, bass.ds(t, 1), 0], rstd[:, bass.ds(t, 1)],
                                      ALU.subtract, ALU.mult).then_inc(xn_ready, 1)

            def split(c, g):
                own = c * 8 + 2 * g
                f, rest, part = qk_f32[:, g % 2, :], qk_rest[:, g % 2, :], qk_part[:, g % 2, :, :]
                dve.wait_ge(f_ready, c * 8 + (2 * (g + 1) + CREDIT[f_ready]))
                dve.tensor_tensor(rest, f, part[:, 0, :], ALU.subtract).then_inc(split_own, 1)
                dve.wait_ge(split_own, own + 1)
                dve.tensor_copy(part[:, 1, :], rest).then_inc(split_own, 1)
                dve.wait_ge(split_own, own + 2)
                dve.tensor_tensor(part[:, 2, :], rest, part[:, 1, :], ALU.subtract).then_inc(split_done, 1)

            def evacuate_v(c):
                for j in range(2):
                    dve.wait_ge(v_ready, c * 2 + (j + 1))
                    dve.tensor_tensor(v_rows[:, bass.ds(c * TPC + 2 * j, 2), :],
                                      ps[:, 4 + j, :].rearrange("p (a c) -> p a c", a=2), bv,
                                      ALU.add).then_inc(v_evac, 1)

            norm_chunk(0)
            with dve.Fori(0, NC - 1) as c:
                split(c, 0)
                split(c, 1)
                dve.wait_ge(t_ready, c + 1)
                norm_chunk(c + 1)
                split(c, 2)
                split(c, 3)
                evacuate_v(c)
            for g in range(4):
                split(NC - 1, g)
            evacuate_v(NC - 1)

            def combine_used(it):
                o = ps[:, 7, 0:P].rearrange("p (i e) -> p i e", i=TPC)
                dve.wait_ge(comb_ready, it + 1)
                dve.reciprocal(rinv[:, :], o[:, :, D]).then_inc(rinv_done, 1)
                dve.wait_ge(rinv_done, it + 1)
                dve.tensor_tensor(attn[:, bass.ds(it * (TPC * D), TPC * D)].rearrange("p (i d) -> p i d", i=TPC),
                                  o[:, :, 0:D], rinv[:, :].unsqueeze(2).to_broadcast([P, TPC, D]),
                                  ALU.mult).then_inc(comb_used, 1)

            def row_max(mi, it):
                dve.wait_ge(negmax_ready, mi + CREDIT[negmax_ready])
                for k in range(16):
                    dve.wait_ge(m_ready, mi * 16 + (k + 1))
                    dve.tensor_reduce(partial[:, k // 4, k % 4:k % 4 + 1], ps[:, 2 * (k % 2):2 * (k % 2) + 2, :], AX.XY,
                                      ALU.max).then_inc(max_used, 1)
                    if k == 5 and it is not None:
                        combine_used(it)
                dve.wait_ge(max_used, mi * 16 + (16 + CREDIT[max_used]))
                dve.wait_ge(nmparts_ready, mi + CREDIT[nmparts_ready])
                dve.tensor_reduce(negmax[:, :], partial[:, :, :], AX.X, ALU.max, negate=True).then_inc(negmax_ready, 1)

            with dve.Fori(0, NC) as c:
                row_max(c, None)
            with dve.Fori(0, H // NB) as r:
                for b in range(NB):
                    with dve.Fori(0, NC) as c:
                        it = r * (NB * NC) + c + b * NC
                        row_max(it + NC, it)
            with dve.Fori(0, NC + 1) as c:
                combine_used(c + (H - 1) * NC)

            for n, (dst, src) in enumerate((
                (keysT.rearrange("p (a n) -> p a n", a=2), ps[:, 4:6, :]),
                (qpT, ps[:, 6, 0:2 * P].rearrange("p (k n) -> p k n", k=CC)),
                (routT, ps[:, 6, 2 * P:2 * P + RD]),
                (u1T, ps[:, 6, 3 * P:4 * P].rearrange("p (k n) -> p k n", k=CC)),
            )):
                if n == 0:
                    dve.wait_ge(w3_t, 1)
                dve.tensor_copy(dst, src).then_inc(w3_e, 1)
            dve.tensor_scalar(rkT[MASKROW:MASKROW + 1, :], rkT[MASKROW:MASKROW + 1, :], float(RD) ** 0.5, None,
                              ALU.mult).then_inc(w3_e, 1)
            dve.wait_ge(w3_t, 2)
            dve.tensor_copy(rkT[0:RD, :].rearrange("p (a n) -> p a n", a=2), ps[0:RD, 0:2, :]).then_inc(w3_e, 1)

            def tile_stats(src, n, own):
                dve.sem_inc(dve_passed, 1)
                for i in range(TPC):
                    last = dve.bn_stats(stats[:, i, :], src(i))
                last.then_inc(own, 1)
                dve.wait_ge(own, n + 1)
                dve.sem_inc(dve_passed, 1)
                for i in range(TPC):
                    last = dve.bn_aggr(mv[:, i, :], stats[:, i, :])
                return last

            def x_tile(c, i):
                return x_sb[:, bass.ds(c * TPC + i, 1), :].rearrange("p a c -> p (a c)")

            def h_tile(c, i):
                return v_rows[:, bass.ds(c * TPC + i, 1), :].rearrange("p a c -> p (a c)")

            with dve.Fori(0, NC) as c:
                for j in range(2):
                    dve.wait_ge(y_psum, c * 2 + (j + 1))
                    dve.tensor_tensor(y[:, 2 * j:2 * j + 2, :], ps[:, 2 + j, :].rearrange("p (a c) -> p a c", a=2),
                                      bproj, ALU.add).then_inc(y_evac, 1)
                dve.wait_ge(y_evac, c * 2 + (2 + CREDIT[y_evac]))
                tile_stats(lambda i: y[:, i, :], c * 7, y_own).then_inc(var_ready, 1)
                dve.wait_ge(rs_ready, c * 2 + 1)
                for i in range(TPC):
                    last = dve.tensor_scalar(y[:, i, :], y[:, i, :], mv[:, i, 0:1], rstd[:, i:i + 1],
                                             ALU.subtract, ALU.mult)
                last.then_inc(y_own, 1)
                dve.wait_ge(y_own, c * 7 + 2)
                xc = x_sb[:, bass.ds(c * TPC, TPC), :]
                dve.tensor_tensor(xc, xc, y, ALU.add).then_inc(y_own, 1)
                dve.wait_ge(y_own, c * 7 + 3)
                tile_stats(lambda i: x_tile(c, i), c * 7 + 3, y_own).then_inc(var_ready, 1)
                dve.wait_ge(rs_ready, c * 2 + 2)
                for i in range(TPC):
                    last = dve.tensor_scalar(h_tile(c, i), x_tile(c, i), mv[:, i, 0:1], rstd[:, i:i + 1],
                                             ALU.subtract, ALU.mult)
                last.then_inc(y_own, 1)
                dve.wait_ge(y_own, c * 7 + 5)
                tile_stats(lambda i: h_tile(c, i), c * 7 + 5, y_own).then_inc(y_own, 1)
                dve.wait_ge(y_own, c * 7 + 7)
                dve.tensor_copy(hvar[:, bass.ds(c * TPC, TPC)], mv[:, 0:TPC, 1]).then_inc(h_ready, 1)

            def take_top(c, i):
                n = c * TPC + i
                sc = ps[:, sc_bank[i % 2]:sc_bank[i % 2] + 2, :]
                dve.wait_ge(sc_psum, n + 1)
                dve.sem_inc(dve_passed, 1)
                dve.max(top8[:, i, :], sc).then_inc(top_ready, 1)
                dve.wait_ge(top_ready, n + 1)
                dve.tensor_scalar(nbias[:, i:i + 1], top8[:, i, 0:1], -RSQ, None, ALU.mult)
                dve.match_replace(picked[i % 2], top8[:, i, :], sc, TAKEN).then_inc(picked_ready, 1)

            def weigh(c, i):
                n = c * TPC + i
                dve.wait_ge(e_ready, n + 1 + CREDIT[e_ready])
                dve.wait_ge(picked_ready, n + 1)
                dve.scalar_tensor_tensor(out=wts_flat[i % 2], in0=picked_flat[i % 2], scalar=TAKEN, in1=wts_flat[i % 2],
                                         op0=ALU.is_equal, op1=ALU.mult,
                                         accum_out=wsum[:, i:i + 1]).then_inc(w_sum, 1)
                dve.wait_ge(w_sum, n + 1)
                dve.reciprocal(wrec[:, i:i + 1], wsum[:, i:i + 1]).then_inc(wr_ready, 1)

            def keep_agg(c, i):
                n = c * TPC + i
                dve.wait_ge(agg_psum, n + 1 + CREDIT[agg_psum])
                dve.wait_ge(wr_ready, n + 1)
                dve.tensor_scalar(agg[:, bass.ds(n, 1), :].rearrange("p a c -> p (a c)"), ps[:, 2 + i % 2, 0:C],
                                  wrec[:, i:i + 1], None, ALU.mult).then_inc(agg_ready, 1)

            with dve.Fori(0, NC) as c:
                dve.wait_ge(l_psum, c + 1)
                dve.tensor_copy(learned[:, bass.ds(c * TPC, TPC)], ps[:, 2, 0:TPC]).then_inc(l_ready, 1)
                take_top(c, 0)
                take_top(c, 1)
                weigh(c, 0)
                take_top(c, 2)
                weigh(c, 1)
                keep_agg(c, 0)
                take_top(c, 3)
                weigh(c, 2)
                keep_agg(c, 1)
                weigh(c, 3)
                keep_agg(c, 2)
                keep_agg(c, 3)

            def step(sem_, n, ins):
                ins.then_inc(sem_, 1)
                dve.wait_ge(sem_, n)

            dve.wait_ge(lv_ready, 1)
            dve.reduce_sum(lvs, lv, axis=AX.X).then_inc(lv_own, 1)
            dve.tensor_scalar(learned, learned, u2b, None, ALU.add).then_inc(g_own, 1)
            dve.wait_ge(lvt_ready, 1)
            dve.tensor_scalar(lvm, ps[:, 2, 0:1], 1.0 / T, 1e-6, ALU.mult, ALU.add).then_inc(g_own, 1)
            dve.wait_ge(g_own, 2)
            dve.reciprocal(lvr, lvm).then_inc(g_own, 1)
            dve.wait_ge(g_own, 3)
            dve.tensor_scalar(lv, lv, lvr, 0.5, ALU.mult, ALU.mult).then_inc(g_own, 1)
            dve.wait_ge(g_e, 1)
            dve.tensor_scalar(gtmp, gtmp, 1.0, None, ALU.add).then_inc(g_own, 1)
            dve.wait_ge(g_own, 5)
            dve.reciprocal(gate, gtmp).then_inc(g_own, 1)
            dve.wait_ge(g_own, 6)
            dve.scalar_tensor_tensor(out=lv, in0=gate, scalar=2.5, in1=lv, op0=ALU.mult, op1=ALU.add).then_inc(g_own, 1)
            dve.wait_ge(g_own, 7)
            dve.tensor_scalar(lv, lv, 0.0, 5.0, ALU.max, ALU.min).then_inc(g_own, 1)
            dve.wait_ge(g_own, 8)
            dve.tensor_scalar(gate, lv, gw, gb, ALU.mult, ALU.add).then_inc(g_a, 1)
            dve.wait_ge(g_e, 2)
            dve.tensor_scalar(gtmp, gtmp, 1.0, None, ALU.add).then_inc(g_own, 1)
            dve.wait_ge(g_own, 9)
            dve.reciprocal(gate, gtmp).then_inc(g_own, 1)
            dve.wait_ge(g_own, 10)

            with dve.Fori(0, NC // 2) as c2:
                for b in range(2):
                    c = c2 * 2 + b
                    own = c2 * 6 + 3 * b
                    dve.wait_ge(res_ready, c2 * 2 + (b + CREDIT[res_ready]))
                    for i in range(TPC):
                        n = c * TPC + i
                        last = dve.scalar_tensor_tensor(
                            out=o2[:, i, :], in0=agg[:, bass.ds(n, 1), :].rearrange("p a c -> p (a c)"),
                            scalar=gate[:, bass.ds(n, 1)], in1=h_tile(c, i), op0=ALU.mult, op1=ALU.add)
                    last.then_inc(o_own, 1)
                    dve.wait_ge(o_own, own + 1)
                    tile_stats(lambda i: o2[:, i, :], own + 1, o_own).then_inc(o_var, 1)
                    dve.wait_ge(o_rs, c + 1)
                    for i in range(TPC):
                        last = dve.tensor_scalar(o2[:, i, :], o2[:, i, :], mv[:, i, 0:1], rstd[:, i:i + 1],
                                                 ALU.subtract, ALU.mult)
                    last.then_inc(o_own, 1)
                    dve.wait_ge(o_own, own + 3)
                    dve.wait_ge(out_done[b], c2 * 16 + 16)
                    dve.tensor_tensor(res[b], o2, x_sb[:, bass.ds(c * TPC, TPC), :], ALU.add).then_inc(res_ready, 1)

        @block.tensor
        def _(pe):
            def transpose_chunk(src, done):
                for i in range(TPC):
                    for k in range(CC):
                        last = pe.transpose(ps[:, k, P * i:P * (i + 1)], src[:, i, P * k:P * (k + 1)], ident[:, :])
                last.then_inc(done, 1)

            def project_qk(c):
                pe.wait_ge(xnT_ready, c + 1)
                for g in range(4):
                    pe.wait_ge(f_ready, c * 8 + 2 * (g + 1))
                    for k in range(CC):
                        last = pe.matmul(ps[:, 2 + g % 2, :], wqkv[:, k, P * g:P * (g + 1)], xnT[:, k, :],
                                         start=(k == 0), stop=(k == CC - 1))
                    last.then_inc(qk_ready, 1)

            def project_v(c):
                for j in range(2):
                    pe.wait_ge(v_evac, c * 2 + (j + 1))
                    for a in range(2):
                        i = 2 * j + a
                        for k in range(CC):
                            last = pe.matmul(ps[:, 4 + j, C * a:C * (a + 1)], xnT[:, k, P * i:P * (i + 1)],
                                             wqkv[:, k, 2 * C:3 * C], start=(k == 0), stop=(k == CC - 1))
                    last.then_inc(v_ready, 1)

            pe.wait_ge(primed, 1)
            pe.wait_ge(w_in, 64)
            pe.wait_ge(xn_ready, TPC)
            transpose_chunk(xn, t_ready)
            with pe.Fori(0, NC - 1) as c:
                project_qk(c)
                pe.wait_ge(xn_ready, c * TPC + 2 * TPC)
                transpose_chunk(xn, t_ready)
                project_v(c)
            project_qk(NC - 1)
            project_v(NC - 1)

            def max_pair(k, mi, b1, c):
                pe.wait_ge(max_used, mi * 16 + (k + 1))
                for e in range(2):
                    last = pe.matmul(ps[:, 2 * (k % 2) + e, :], q_stack[0:ROWS, b1, bass.ds(c * CH + (k // 4) * P, P)],
                                     k_stack[0:ROWS, b1, CH * (2 * (k % 4) + e):CH * (2 * (k % 4) + e + 1)],
                                     start=True, stop=True)
                last.then_inc(m_ready, 1)

            def score(g, i, it, b, c):
                pe.wait_ge(exp_done, it * NT + (4 * g + i + 1))
                pe.matmul(ps[:, 4 + i % 2, :], k_stack[0:ROWS + MROWS, b, P * (4 * g + i):P * (4 * g + i + 1)],
                          q_stack[0:ROWS + MROWS, b, bass.ds(c * CH, CH)], start=True, stop=True).then_inc(s_ready, 1)

            def weighted_values(g, it, b):
                pe.wait_ge(exp_done, it * NT + (4 * g + 4 + CREDIT[exp_done]))
                if g == 0:
                    pe.wait_ge(o_evac, it + 1)
                for j in range(4):
                    last = pe.matmul(ps[32 * j:32 * j + 32, 6, :], v_head[:, b, 4 * g + j, :], probs[:, g % 4, j, :],
                                     start=(g == 0), stop=(g == KG - 1))
                last.then_inc(pv_done, 1)

            def combine(it, rows_done):
                pe.wait_ge(o_evac, it + 1)
                pe.wait_ge(mrow_done, rows_done)
                pe.wait_ge(comb_used, it + 1)
                for i in range(TPC):
                    last = pe.matmul(ps[:, 7, 32 * i:32 * i + D + 1], o_sb[:, P * i:P * (i + 1)], sel[:, :],
                                     start=True, stop=True)
                last.then_inc(comb_ready, 1)

            def max_row(h, b, c, made, used):
                pe.wait_ge(nmparts_ready, made + CREDIT[nmparts_ready])
                pe.wait_ge(comb_used, used)
                for i in range(TPC):
                    last = pe.matmul(ps[0:MROWS, 7, P * i:P * (i + 1)], nm_all[:, b, bass.ds(c * TPC + i, 1), :].rearrange("p a r -> p (a r)"),
                                     ident_bf[:, :], start=True, stop=True)
                last.then_inc(mrow_ready, 1)

            def attend(h, b, c, b1):
                it = h * NC + c
                rows = h * (NC + 1) + c + 1
                pe.wait_ge(mrow_done, rows)
                for g in range(KG):
                    score(g, 0, it, b, c)
                    score(g, 1, it, b, c)
                    if b1 is not None:
                        max_pair(2 * g, it + NC, b1, c)
                    if g:
                        weighted_values(g - 1, it, b)
                    score(g, 2, it, b, c)
                    score(g, 3, it, b, c)
                    if b1 is not None:
                        max_pair(2 * g + 1, it + NC, b1, c)
                    if g == 1:
                        combine(it, rows)
                    if g == 4:
                        max_row(h, b, c + 1, h * NC + NC, it + 2)
                weighted_values(KG - 1, it, b)

            pe.wait_ge(stack_in[0], 16 * 12)
            with pe.Fori(0, NC) as c:
                for k in range(16):
                    max_pair(k, c, 0, c)
            with pe.Fori(0, H // NB) as r:
                for b in range(NB):
                    h = r * NB + b
                    b1 = (b + 1) % NB
                    pe.wait_ge(stack_in[b1], (r + 1 + (b + 1) // NB) * (16 * 12))
                    pe.wait_ge(vhead_ready, h + 1)
                    max_row(h, b, 0, h * NC + 1, h * NC + 1)
                    with pe.Fori(0, NC) as c:
                        attend(h, b, c, b1)
            h = H - 1
            pe.wait_ge(vhead_ready, h + 1)
            max_row(h, 0, 0, h * NC + 1, h * NC + 1)
            with pe.Fori(0, NC) as c:
                attend(h, 0, c, None)
            combine(ITS, H * (NC + 1))

            pe.wait_ge(w3_in, 16 * W3_LOADS)
            pe.wait_ge(w3_init, 4)
            for v in range(NV):
                pe.transpose(ps[:, 4 + v // 4, P * (v % 4):P * (v % 4 + 1)], keys[:, v, :], ident[:, :])
            for k in range(CC):
                pe.transpose(ps[:, 6, P * k:P * (k + 1)], qpw[:, P * k:P * (k + 1)], ident[:, :])
                pe.transpose(ps[:, 6, 3 * P + F1 * k:3 * P + F1 * (k + 1)], u1w[0:F1, P * k:P * (k + 1)], ident[0:F1, 0:F1])
            pe.transpose(ps[:, 6, 2 * P:2 * P + RD], routw[0:RD, :], ident[0:RD, 0:RD]).then_inc(w3_t, 1)
            pe.wait_ge(w3_e, 4)
            for a in range(2):
                last = pe.matmul(ps[0:RD, a, :], routT, keysT[:, CH * a:CH * (a + 1)], start=True, stop=True)
            last.then_inc(w3_t, 1)
            pe.wait_ge(w3_e, 6)
            with pe.Fori(0, NC) as c:
                pe.wait_ge(stage_ready, c + 1)
                transpose_chunk(stage, aT_psum)
                pe.wait_ge(aT_ready, c + 1)
                for j in range(2):
                    pe.wait_ge(y_evac, c * 2 + (j + 1))
                    for a in range(2):
                        i = 2 * j + a
                        for k in range(CC):
                            last = pe.matmul(ps[:, 2 + j, C * a:C * (a + 1)], aT[:, k, P * i:P * (i + 1)], wproj[:, k, :],
                                             start=(k == 0), stop=(k == CC - 1))
                    last.then_inc(y_psum, 1)

            def lookup_scores(c, i):
                n = c * TPC + i
                if i:
                    pe.wait_ge(e_ready, n + 1)
                for a in range(2):
                    last = pe.matmul(ps[:, sc_bank[i % 2] + a, :], rqT[0:MASKROW + 1, P * i:P * (i + 1)],
                                     rkT[0:MASKROW + 1, CH * a:CH * (a + 1)], start=True, stop=True)
                last.then_inc(sc_psum, 1)

            pe.wait_ge(y_evac, 2 * NC + CREDIT[y_evac])
            with pe.Fori(0, NC) as c:
                pe.wait_ge(stage_ready, c + 1 + NC)
                pe.wait_ge(e_ready, c * TPC + CREDIT[e_ready])
                transpose_chunk(stage, hT_psum)
                pe.wait_ge(hT_ready, c + 1)
                pe.wait_ge(agg_ready, c * TPC + CREDIT[agg_ready])
                for k in range(CC):
                    last = pe.matmul(ps[0:F1, 3, :], u1T[:, k, :], hT[:, k, :], start=(k == 0), stop=(k == CC - 1))
                last.then_inc(u_psum, 1)
                for k in range(CC):
                    last = pe.matmul(ps[:, 2, :], qpT[:, k, :], hT[:, k, :], start=(k == 0), stop=(k == CC - 1))
                last.then_inc(qy_psum, 1)
                pe.wait_ge(u_ready, c + 1)
                pe.wait_ge(qy_ready, c + 1)
                pe.matmul(ps[0:RD, 3, :], routT, queryT, start=True, stop=True).then_inc(rq_psum, 1)
                for i in range(TPC):
                    last = pe.matmul(ps[:, 2, i:i + 1], g1T[0:F1, P * i:P * (i + 1)], u2w[0:F1, :], start=True, stop=True)
                last.then_inc(l_psum, 1)
                pe.wait_ge(rq_ready, c + 1)
                lookup_scores(c, 0)
                pe.wait_ge(l_ready, c + 1 + CREDIT[l_ready])
                for i in range(TPC):
                    n = c * TPC + i
                    if i < TPC - 1:
                        lookup_scores(c, i + 1)
                    pe.wait_ge(wr_ready, n + 1)
                    pe.wait_ge(wT_ready, n + CREDIT[wT_ready])
                    for v in range(NV):
                        last = pe.transpose(ps[:, 6 + v // 4, P * (v % 4):P * (v % 4 + 1)],
                                            wts_flat[i % 2][:, P * v:P * (v + 1)], ident[:, :])
                    last.then_inc(wT_psum, 1)
                    pe.wait_ge(wT_ready, n + 1 + CREDIT[wT_ready])
                    if i >= 2:
                        pe.wait_ge(agg_ready, n - 1 + CREDIT[agg_ready])
                    for v in range(NV):
                        last = pe.matmul(ps[:, 2 + i % 2, 0:C], wT[:, v, :], values[:, v, :],
                                         start=(v == 0), stop=(v == NV - 1))
                    last.then_inc(agg_psum, 1)
            pe.wait_ge(lv_own, 1)
            pe.wait_ge(agg_ready, NT + CREDIT[agg_ready])
            pe.matmul(ps[:, 2, 0:1], ones, lvs, start=True, stop=True).then_inc(lvt_ready, 1)


INPUTS = ["L0_attn_x", "L0_attn_w_qkv", "L0_attn_b_qkv", "L0_attn_w_proj", "L0_attn_b_proj", "L0_ffn_q_proj_w",
          "L0_ffn_router_w", "L0_ffn_aux_keys", "L0_ffn_aux_values", "L0_ffn_reliability_mask", "L0_ffn_unc_w1",
          "L0_ffn_unc_b1", "L0_ffn_unc_w2", "L0_ffn_unc_b2", "L0_ffn_gate_w1", "L0_ffn_gate_bias"]


def kernel(**inputs):
    import numpy as np
    import concourse.bacc as bacc
    from concourse.bass_utils import run_bass_kernel_spmd

    nc = bacc.Bacc("TRN2", target_bir_lowering=False, num_devices=1)
    arrays, args = {}, []
    for name in INPUTS:
        a = np.ascontiguousarray(inputs[name])
        arrays[name] = a
        args.append(nc.dram_tensor(name, a.shape, mybir.dt.from_np(a.dtype), kind="ExternalInput").ap())
    shape = arrays["L0_attn_x"].shape
    args.append(nc.dram_tensor("out", shape, F32, kind="ExternalOutput").ap())
    sandwich_kernel(nc, *args)
    result = run_bass_kernel_spmd(nc, [arrays], core_ids=[0])
    return result.results[0]["out"]
```

```python
from contextlib import ExitStack

import concourse.bass as bass
from concourse import mybir

F32 = mybir.dt.float32
BF16 = mybir.dt.bfloat16
ALU = mybir.AluOpType
ACT = mybir.ActivationFunctionType
AX = mybir.AxisListType

P = 128
CH = 512
EPS = 1e-5
NB = 3
SLOT_Q = [0, 0, 1, 0, 1, 2]
SLOT_K = [0, 1, 0, 2, 1, 0]
TAKEN = -3.0e38


def sandwich_kernel(nc, x, w_qkv, b_qkv, w_proj, b_proj, q_proj_w, router_w, aux_keys, aux_values,
                    reliability_mask, unc_w1, unc_b1, unc_w2, unc_b2, gate_w1, gate_bias, out):
    _, T, C = x.shape
    H = 16
    D = C // H
    NT = T // P
    NC = T // CH
    TPC = CH // P
    CC = C // P
    BOT = q_proj_w.shape[0]
    RD = router_w.shape[0]
    N = aux_keys.shape[0]
    NV = N // P
    F1 = unc_w1.shape[0]
    SCALE = float(D) ** -0.5
    RSQ = float(RD) ** -0.5
    ROWS = 6 * D
    MROWS = 3
    KG = NT // 4
    AHEAD = 2
    ITS = H * NC
    MASKROW = 64
    assert ROWS == 96 and C == 256 and T == 4096 and BOT == P and RD <= MASKROW and N == 1024

    x_t = x[0].rearrange("(t p) c -> p t c", p=P)
    out_t = out[0].rearrange("(t p) c -> p t c", p=P)
    parts_dram = nc.dram_tensor("qk_parts", (2, 3, C, T), BF16, kind="Internal").ap()

    with ExitStack() as ctx:
        def sb(name, shape, dt=F32):
            return ctx.enter_context(nc.sbuf_tensor(name, shape, dt))

        def sem(name):
            return ctx.enter_context(nc.semaphore(name))

        ps = ctx.enter_context(nc.psum_tensor("ps", [P, 8, CH], F32))

        x_sb = sb("x_sb", [P, NT, C])
        v_all = sb("v_all", [P, NT * C])
        attn = sb("attn", [P, NC * TPC * C + 4 * D])
        work = sb("work", [P, 8192])
        q_raw = sb("q_raw", [P, NB * T // 2])
        k_raw = sb("k_raw", [P, NB * T // 2])
        v_head = sb("v_head", [P, NB, NT, 32])
        o_sb = sb("o_sb", [P, CH])
        ident = sb("ident", [P, P])
        ident_bf = sb("ident_bf", [P, P], BF16)
        sel = sb("sel", [P, D + 1])
        stats = sb("stats", [P, NT, 6])
        mv = sb("mv", [P, NT, 2])
        rstd = sb("rstd", [P, NT])
        veps = sb("veps", [P, NT])
        hvar = sb("hvar", [P, NT])
        minus_half = sb("minus_half", [P, NT])
        partial = sb("partial", [P, TPC, 4])
        negmax = sb("negmax", [P, TPC])
        nm_rest = sb("nm_rest", [P, 2, TPC])
        nm_parts = sb("nm_parts", [P, TPC, MROWS], BF16)
        rinv = sb("rinv", [P, TPC])

        q_stack = q_raw[:, :].bitcast(BF16).rearrange("p (b t) -> p b t", b=NB)
        k_stack = k_raw[:, :].bitcast(BF16).rearrange("p (b t) -> p b t", b=NB)
        v_rows = v_all[:, :].rearrange("p (t c) -> p t c", c=C)

        xn = work[:, 0:1024].rearrange("p (t c) -> p t c", t=TPC)
        xnT = work[:, 1024:2048].rearrange("p (k t) -> p k t", k=CC)
        wqkv = work[:, 2048:3584].rearrange("p (k n) -> p k n", k=CC)
        qk_f32 = work[:, 3584:4608].rearrange("p (b t) -> p b t", b=2)
        qk_rest = work[:, 4608:5632].rearrange("p (b t) -> p b t", b=2)
        qk_part = work[:, 5632:7168].bitcast(BF16).rearrange("p (b r t) -> p b r t", b=2, r=3)
        bv = work[:, 7168:7680].rearrange("p (a c) -> p a c", a=2)
        bqk = work[:, 7680:7684]
        probs = work[:, :].rearrange("p (r j t) -> p r j t", r=4, j=4)
        stage_a = work[:, 0:1024].rearrange("p (t c) -> p t c", t=TPC)
        aT = work[:, 1024:2048].rearrange("p (k t) -> p k t", k=CC)
        y = work[:, 2048:3072].rearrange("p (t c) -> p t c", t=TPC)
        stage_h = work[:, 3072:4096].rearrange("p (t c) -> p t c", t=TPC)
        hT = work[:, 4096:5120].rearrange("p (k t) -> p k t", k=CC)
        queryT = work[:, 5120:5632]
        rqT = work[:, 5632:6144]
        g1T = work[:, 6144:6656]
        o2 = work[:, 0:1024].rearrange("p (t c) -> p t c", t=TPC)
        res = [work[:, 1024 * (b + 1):1024 * (b + 2)].rearrange("p (t c) -> p t c", t=TPC) for b in range(2)]
        picked_flat = [q_raw[:, 1024 * (b + 3):1024 * (b + 4)] for b in range(2)]
        wts_flat = [k_raw[:, 1024 * (b + 3):1024 * (b + 4)] for b in range(2)]
        picked = [v.rearrange("p (a n) -> p a n", a=2) for v in picked_flat]
        wts = [v.rearrange("p (a n) -> p a n", a=2) for v in wts_flat]
        sc_bank = [4, 6]
        wproj = k_raw[:, 0:512].rearrange("p (k n) -> p k n", k=CC)
        bproj = k_raw[:, 512:1024].rearrange("p (a c) -> p a c", a=2)
        values = k_raw[:, 1024:3072].rearrange("p (v c) -> p v c", v=NV)
        keys = k_raw[:, 3072:4096].rearrange("p (v c) -> p v c", v=NV)
        keysT = k_raw[:, 4096:5120]
        rkT = k_raw[:, 5120:6144]
        qpw = q_raw[:, 0:256]
        qpT = q_raw[:, 256:512].rearrange("p (k n) -> p k n", k=CC)
        routw = q_raw[:, 512:640]
        routT = q_raw[:, 640:640 + RD]
        u1w = q_raw[:, 704:960]
        u1T = q_raw[:, 960:1088].rearrange("p (k n) -> p k n", k=CC)
        small = q_raw[:, 1088:1152]
        u1b, u2w, u2b, gw, gb = (small[:, i:i + 1] for i in range(5))
        lvs, lvm, lvr = (small[:, i:i + 1] for i in range(5, 8))
        ones = q_raw[:, 1152:1280]
        top8 = q_raw[:, 1440:1472].rearrange("p (i e) -> p i e", i=TPC)
        nbias = q_raw[:, 1280:1284]
        wsum = q_raw[:, 1284:1288]
        wrec = q_raw[:, 1288:1292]
        lv = q_raw[:, 1312:1344]
        learned = q_raw[:, 1344:1376]
        gate = q_raw[:, 1376:1408]
        gtmp = q_raw[:, 1408:1440]
        wT = q_raw[:, 1536:2560].rearrange("p (v t) -> p v t", v=NV)
        wT2 = q_raw[:, 1536:2560].rearrange("p (a n) -> p a n", a=2)

        attn_h = attn[:, 4 * D:].rearrange("p (h t d) -> p h t d", h=H, t=NT)

        def agg_tile(n):
            return attn_h[:, :, bass.ds(n, 1), :].rearrange("p h a d -> p (h a) d")

        x_in = [sem(f"x_in{c}") for c in range(NC)]
        w_in = sem("w_in")
        primed = sem("primed")
        consts = sem("consts")
        st_done = sem("st_done")
        rstd_done = sem("rstd_done")
        pool_own = sem("pool_own")
        xn_ready = sem("xn_ready")
        t_ready = sem("t_ready")
        xnT_ready = sem("xnT_ready")
        qk_ready = sem("qk_ready")
        f_ready = sem("f_ready")
        split_own = sem("split_own")
        split_done = sem("split_done")
        parts_out = [sem("parts_out0"), sem("parts_out1")]
        v_ready = sem("v_ready")
        v_evac = sem("v_evac")
        stack_in = [sem(f"stack_in{b}") for b in range(NB)]
        s_ready = sem("s_ready")
        exp_done = sem("exp_done")
        m_ready = sem("m_ready")
        max_used = sem("max_used")
        negmax_ready = sem("negmax_ready")
        nmparts_ready = sem("nmparts_ready")
        vhead_ready = sem("vhead_ready")
        pv_done = sem("pv_done")
        o_evac = sem("o_evac")
        comb_ready = sem("comb_ready")
        rinv_done = sem("rinv_done")
        comb_used = sem("comb_used")
        mrow_ready = sem("mrow_ready")
        mrow_done = sem("mrow_done")
        dve_passed = sem("dve_passed")
        pool_passed = sem("pool_passed")
        pe_passed = sem("pe_passed")
        w3_in = sem("w3_in")
        w3_init = sem("w3_init")
        w3_t = sem("w3_t")
        w3_e = sem("w3_e")
        pow_own = sem("pow_own")
        stage_a_ready = sem("stage_a_ready")
        stage_h_ready = sem("stage_h_ready")
        aT_psum = sem("aT_psum")
        aT_ready = sem("aT_ready")
        y_psum = sem("y_psum")
        y_own = sem("y_own")
        y_evac = sem("y_evac")
        var_ready = sem("var_ready")
        rs_ready = sem("rs_ready")
        h_ready = sem("h_ready")
        hT_psum = sem("hT_psum")
        hT_ready = sem("hT_ready")
        qy_psum = sem("qy_psum")
        qy_ready = sem("qy_ready")
        rq_psum = sem("rq_psum")
        rq_ready = sem("rq_ready")
        u_psum = sem("u_psum")
        u_ready = sem("u_ready")
        l_psum = sem("l_psum")
        l_ready = sem("l_ready")
        sc_psum = sem("sc_psum")
        top_ready = sem("top_ready")
        nb_ready = sem("nb_ready")
        picked_ready = sem("picked_ready")
        e_ready = sem("e_ready")
        w_sum = sem("w_sum")
        wr_ready = sem("wr_ready")
        wT_psum = sem("wT_psum")
        wT_ready = sem("wT_ready")
        agg_psum = sem("agg_psum")
        agg_ready = sem("agg_ready")
        lv_ready = sem("lv_ready")
        lv_own = sem("lv_own")
        lvt_ready = sem("lvt_ready")
        g_own = sem("g_own")
        g_e = sem("g_e")
        g_a = sem("g_a")
        o_own = sem("o_own")
        o_var = sem("o_var")
        o_rs = sem("o_rs")
        res_ready = sem("res_ready")
        out_done = [sem("out_done0"), sem("out_done1")]

        CREDIT = {exp_done: 2, max_used: 2, pv_done: 4, o_evac: 1, comb_used: 1, nmparts_ready: 1, negmax_ready: 1, res_ready: 1, mrow_ready: 1, y_psum: 1,
                  f_ready: 4, split_done: 2, v_evac: 2, aT_psum: 1, hT_psum: 1, y_evac: 2, e_ready: 2, wT_ready: 1,
                  agg_ready: 2, l_ready: 1, agg_psum: 1,
                  wT_psum: 2}

        block = ctx.enter_context(nc.Block())

        @block.sync
        def _(sp):
            for c in range(NC):
                sp.dma_start(x_sb[:, TPC * c:TPC * (c + 1), :], x_t[:, TPC * c:TPC * (c + 1), :]).then_inc(x_in[c], 16)
            with sp.Fori(0, NC) as c:
                for g in range(4):
                    sp.wait_ge(split_done, c * 4 + (g + 1 + CREDIT[split_done]))
                    dst = parts_dram[g // 2, :, (g % 2) * P:(g % 2 + 1) * P, bass.ds(c * CH, CH)]
                    sp.dma_start(dst.rearrange("r f t -> f r t"), qk_part[:, g % 2, :, :]).then_inc(parts_out[g % 2], 16)
            for b in range(2):
                sp.wait_ge(parts_out[b], 16 * (2 * NC + 1))

            def load_stack(h, b):
                for s in range(6):
                    for stack, qk, part in ((k_stack, 1, SLOT_K[s]), (q_stack, 0, SLOT_Q[s])):
                        sp.dma_start(stack[D * s:D * (s + 1), b, 0:T], parts_dram[qk, part, bass.ds(h * D, D), :]
                                     ).then_inc(stack_in[b], 16)

            for b in range(NB):
                load_stack(b, b)
            with sp.Fori(1, H // NB) as r:
                for b in range(NB):
                    sp.wait_ge(pv_done, r * (NB * NC * KG) + ((b - 2) * NC * KG + CREDIT[pv_done]))
                    load_stack(r * NB + b, b)
            sp.wait_ge(pv_done, (H - 3) * NC * KG + CREDIT[pv_done])
            load_stack(H - 1, (H - 1) % NB)

            sp.wait_ge(pv_done, ITS * KG + CREDIT[pv_done])
            sp.wait_ge(w3_init, 3)
            for dst, src in (
                (wproj, w_proj.rearrange("(k p) n -> p k n", p=P)),
                (bproj[:, 0, :], b_proj.partition_broadcast(P)),
                (bproj[:, 1, :], b_proj.partition_broadcast(P)),
                (keys, aux_keys.rearrange("(v p) d -> p v d", p=P)),
                (qpw, q_proj_w),
                (routw[0:RD, :], router_w),
                (u1w[0:F1, :], unc_w1),
                (u1b[0:F1, :], unc_b1.rearrange("(f a) -> f a", a=1)),
                (u2w[0:F1, :], unc_w2.rearrange("a f -> f a")),
                (u2b, unc_b2.partition_broadcast(P)),
                (gw, gate_w1.partition_broadcast(P)),
                (gb, gate_bias.partition_broadcast(P)),
                (rkT[MASKROW:MASKROW + 1, :], reliability_mask.rearrange("(a n) -> a n", a=1)),
                (values, aux_values.rearrange("(v p) d -> p v d", p=P)),
            ):
                sp.dma_start(dst, src, allow_slow_non_contiguous=True).then_inc(w3_in, 16)

            with sp.Fori(0, NC // 2) as c2:
                for b in range(2):
                    sp.wait_ge(res_ready, c2 * 2 + (b + 1 + CREDIT[res_ready]))
                    sp.dma_start(out_t[:, bass.ds(c2 * (2 * TPC) + b * TPC, TPC), :], res[b]).then_inc(out_done[b], 16)
            for b in range(2):
                sp.wait_ge(out_done[b], 16 * (NC // 2 + 1))

        W3_LOADS = 14

        @block.gpsimd
        def _(pool):
            pool.dma_start(wqkv, w_qkv.rearrange("(k p) n -> p k n", p=P)).then_inc(w_in, 16)
            pool.dma_start(bqk, b_qkv[0:2 * C].rearrange("(g p) -> p g", p=P), allow_slow_non_contiguous=True).then_inc(w_in, 16)
            for a in range(2):
                pool.dma_start(bv[:, a, :], b_qkv[2 * C:3 * C].partition_broadcast(P)).then_inc(w_in, 16)
            pool.memset(minus_half[:], -0.5).then_inc(consts, 1)
            pool.memset(ident[:], 0.0).then_inc(consts, 1)
            pool.memset(sel[:], 0.0).then_inc(consts, 1)
            pool.memset(o_sb[:], 1.0).then_inc(consts, 1)
            pool.wait_ge(consts, 4)
            pool.memset(k_stack[ROWS:ROWS + MROWS, :, :], 1.0).then_inc(consts, 1)
            pool.wait_ge(consts, 5)
            pool.memset(v_head[:], 0.0).then_inc(consts, 1)
            pool.wait_ge(consts, 6)
            pool.affine_select(out=ident[:], in_=ident[:], compare_op=ALU.not_equal, fill=1.0, base=0,
                               pattern=[[-1, P]], channel_multiplier=1).then_inc(consts, 1)
            pool.memset(v_head[:, :, :, D], 1.0).then_inc(consts, 1)
            pool.wait_ge(consts, 8)
            for j in range(4):
                pool.affine_select(out=sel[:], in_=sel[:], compare_op=ALU.not_equal, fill=1.0, base=-32 * j,
                                   pattern=[[-1, D + 1]], channel_multiplier=1).then_inc(consts, 1)
                pool.wait_ge(consts, 9 + j)
            pool.tensor_copy(ident_bf[:], ident[:]).then_inc(consts, 1)
            pool.wait_ge(consts, 13)
            for s, n in CREDIT.items():
                if n:
                    pool.sem_inc(s, n)
            for s in parts_out + out_done:
                pool.sem_inc(s, 16)
            pool.sem_inc(primed, 1)

            pool.wait_ge(st_done, 2 * NT)
            pool.tensor_scalar(veps[:, :], mv[:, :, 1], EPS, None, ALU.add).then_inc(pool_own, 1)
            pool.wait_ge(pool_own, 1)
            pool.tensor_tensor(rstd[:, :], veps[:, :], minus_half[:, :], ALU.pow).then_inc(rstd_done, 1)

            def copy_v(h, b):
                pool.tensor_copy(v_head[:, b, :, 0:D], v_rows[:, :, bass.ds(h * D, D)]).then_inc(vhead_ready, 1)

            pool.wait_ge(v_evac, 2 * NC + CREDIT[v_evac])
            copy_v(0, 0)

            def split_max(mi):
                pool.wait_ge(negmax_ready, mi + 1 + CREDIT[negmax_ready])
                pool.wait_ge(mrow_ready, mi + CREDIT[mrow_ready])
                pool.sem_inc(pool_passed, 1)
                pool.tensor_copy(nm_parts[:, :, 0], negmax[:, :]).then_inc(pool_own, 1)
                pool.wait_ge(pool_own, mi * 4 + 2)
                pool.tensor_tensor(nm_rest[:, 0, :], negmax[:, :], nm_parts[:, :, 0], ALU.subtract).then_inc(pool_own, 1)
                pool.wait_ge(pool_own, mi * 4 + 3)
                pool.sem_inc(pool_passed, 1)
                pool.tensor_copy(nm_parts[:, :, 1], nm_rest[:, 0, :]).then_inc(pool_own, 1)
                pool.wait_ge(pool_own, mi * 4 + 4)
                pool.tensor_tensor(nm_rest[:, 1, :], nm_rest[:, 0, :], nm_parts[:, :, 1], ALU.subtract).then_inc(pool_own, 1)
                pool.wait_ge(pool_own, mi * 4 + 5)
                pool.sem_inc(pool_passed, 1)
                pool.tensor_copy(nm_parts[:, :, 2], nm_rest[:, 1, :]).then_inc(nmparts_ready, 1)

            with pool.Fori(0, AHEAD) as c:
                split_max(c)
            with pool.Fori(0, H // NB) as r:
                for b in range(NB):
                    pool.wait_ge(pv_done, r * (NB * NC * KG) + (b * NC * KG + CREDIT[pv_done]))
                    pool.sem_inc(pool_passed, 1)
                    copy_v(r * NB + (b + 1), (b + 1) % NB)
                    with pool.Fori(0, NC) as c:
                        split_max(r * (NB * NC) + c + (b * NC + AHEAD))
            with pool.Fori(ITS - NC + AHEAD, ITS) as c:
                split_max(c)

            pool.wait_ge(pv_done, ITS * KG + CREDIT[pv_done])
            pool.memset(rkT, 0.0).then_inc(w3_init, 1)
            pool.memset(ones, 1.0).then_inc(w3_init, 1)
            pool.memset(rqT, 0.0).then_inc(w3_init, 1)
            pool.wait_ge(w3_init, 3)
            pool.memset(rqT[MASKROW:MASKROW + 1, :], 1.0).then_inc(w3_init, 1)
            pool.wait_ge(w3_init, 4)

            def powers(n, rs):
                pool.sem_inc(pool_passed, 1)
                pool.tensor_scalar(veps[:, 0:TPC], mv[:, 0:TPC, 1], EPS, None, ALU.add).then_inc(pow_own, 1)
                pool.wait_ge(pow_own, n)
                pool.tensor_tensor(rstd[:, 0:TPC], veps[:, 0:TPC], minus_half[:, 0:TPC], ALU.pow).then_inc(rs, 1)

            def stage_attn(c):
                pool.wait_ge(aT_psum, c + CREDIT[aT_psum])
                pool.sem_inc(pool_passed, 1)
                for i in range(TPC):
                    last = pool.tensor_copy(stage_a[:, i, :].rearrange("p (h d) -> p h d", h=H),
                                            attn_h[:, :, bass.ds(c * TPC + i, 1), :].rearrange("p h a d -> p (h a) d"))
                last.then_inc(stage_a_ready, 1)

            def block_powers(c):
                for k in range(2):
                    pool.wait_ge(var_ready, c * 2 + (k + 1))
                    powers(c * 2 + (k + 1), rs_ready)

            def stage_block(c):
                pool.wait_ge(h_ready, c + 1)
                pool.wait_ge(hT_psum, c + CREDIT[hT_psum])
                pool.sem_inc(pool_passed, 1)
                pool.tensor_copy(stage_h, v_rows[:, bass.ds(c * TPC, TPC), :]).then_inc(stage_h_ready, 1)

            pool.wait_ge(comb_used, ITS + 1 + CREDIT[comb_used])
            stage_attn(0)
            stage_attn(1)
            block_powers(0)
            stage_block(0)
            stage_attn(2)
            with pool.Fori(1, NC - 2) as c:
                block_powers(c)
                stage_block(c)
                stage_attn(c + 2)
            for c in range(NC - 2, NC):
                block_powers(c)
                stage_block(c)
            with pool.Fori(0, NC) as c:
                pool.wait_ge(o_var, c + 1)
                powers(c + (2 * NC + 1), o_rs)

        @block.scalar
        def _(act):
            act.wait_ge(w_in, 64)

            def move_xnT(c):
                act.wait_ge(t_ready, c + 1)
                act.activation(xnT, ps[:, 0:2, :], ACT.Copy).then_inc(xnT_ready, 1)

            def evacuate_qk(c):
                for g in range(4):
                    act.wait_ge(qk_ready, c * 4 + (g + 1))
                    act.wait_ge(split_done, c * 4 + (g + 1))
                    act.wait_ge(parts_out[g % 2], c * 32 + 16 * (g // 2 + 1))
                    act.activation(qk_f32[:, g % 2, :], ps[:, 2 + g % 2, :], ACT.Identity,
                                   bias=bqk[:, g:g + 1]).then_inc(f_ready, 1)
                    act.activation(qk_part[:, g % 2, 0, :], ps[:, 2 + g % 2, :], ACT.Identity,
                                   bias=bqk[:, g:g + 1]).then_inc(f_ready, 1)

            move_xnT(0)
            with act.Fori(0, NC - 1) as c:
                evacuate_qk(c)
                act.wait_ge(v_ready, c * 2 + 2)
                move_xnT(c + 1)
            evacuate_qk(NC - 1)

            def move_max_row(b, c, n):
                act.wait_ge(mrow_ready, n + 1 + CREDIT[mrow_ready])
                act.activation(q_stack[ROWS:ROWS + MROWS, b, bass.ds(c * CH, CH)], ps[0:MROWS, 7, :],
                               ACT.Copy).then_inc(mrow_done, 1)

            def exponential(g, i, it):
                if i == 0:
                    act.wait_ge(pv_done, it * KG + (g + 1))
                act.wait_ge(s_ready, it * NT + (4 * g + i + 1))
                act.activation(probs[:, g % 4, i, :], ps[:, 4 + i % 2, :], ACT.Exp, scale=SCALE).then_inc(exp_done, 1)

            def attend(it, next_row):
                for g in range(KG):
                    for i in range(4):
                        if g == 5 and i == 2 and next_row:
                            move_max_row(*next_row, it + 1)
                        if g or i >= 2:
                            exponential(g, i, it)
                if next_row:
                    exponential(0, 0, it + 1)
                    exponential(0, 1, it + 1)
                act.wait_ge(pv_done, it * KG + (KG + CREDIT[pv_done]))
                act.wait_ge(comb_ready, it + 1)
                act.activation(o_sb[:, :], ps[:, 6, :], ACT.Copy).then_inc(o_evac, 1)

            move_max_row(0, 0, 0)
            exponential(0, 0, 0)
            exponential(0, 1, 0)
            with act.Fori(0, H // NB) as r:
                for b in range(NB):
                    first = r * (NB * NC) + b * NC
                    with act.Fori(0, NC - 1) as c:
                        attend(first + c, (b, c + 1))
                    attend(first + (NC - 1), ((b + 1) % NB, 0))
            with act.Fori(0, NC - 1) as c:
                attend(c + (H - 1) * NC, (0, c + 1))
            attend(ITS - 1, None)

            def move_aT(c):
                act.wait_ge(aT_psum, c + 1 + CREDIT[aT_psum])
                act.wait_ge(y_psum, c * 2 + CREDIT[y_psum])
                act.activation(aT, ps[:, 0:2, :], ACT.Copy).then_inc(aT_ready, 1)

            def move_wT(c, i):
                n = c * TPC + i
                act.wait_ge(wT_psum, n + 1 + CREDIT[wT_psum])
                act.wait_ge(agg_psum, n + CREDIT[agg_psum])
                act.activation(wT2, ps[:, 0:2, :], ACT.Copy).then_inc(wT_ready, 1)

            def exponentials(c, i):
                n = c * TPC + i
                act.wait_ge(picked_ready, n + 1)
                act.wait_ge(wT_psum, n - 1 + CREDIT[wT_psum])
                act.activation(wts[i % 2], ps[:, sc_bank[i % 2]:sc_bank[i % 2] + 2, :], ACT.Exp,
                               bias=nbias[:, i:i + 1], scale=RSQ).then_inc(e_ready, 1)

            def ffn_chunk(c, two_ahead):
                act.wait_ge(hT_psum, c + 1 + CREDIT[hT_psum])
                act.activation(hT, ps[:, 0:2, :], ACT.Copy).then_inc(hT_ready, 1)
                act.wait_ge(qy_psum, c + 1)
                act.activation(queryT, ps[:, 4, :], ACT.Copy).then_inc(qy_ready, 1)
                act.wait_ge(rq_psum, c + 1)
                act.activation(rqT[0:RD, :], ps[0:RD, 6, :], ACT.Copy).then_inc(rq_ready, 1)
                act.wait_ge(u_psum, c + 1)
                act.activation(g1T[0:F1, :], ps[0:F1, 7, :], ACT.Gelu, bias=u1b[0:F1, :]).then_inc(u_ready, 1)
                exponentials(c, 0)
                if two_ahead:
                    move_aT(c + 2)
                move_wT(c, 0)
                for i in range(1, TPC):
                    exponentials(c, i)
                    move_wT(c, i)

            move_aT(0)
            move_aT(1)
            with act.Fori(0, NC - 2) as c:
                ffn_chunk(c, True)
            for c in range(NC - 2, NC):
                ffn_chunk(c, False)
            act.activation(lv, hvar[:, :], ACT.Ln, bias=1.0).then_inc(lv_ready, 1)
            act.wait_ge(g_own, 3)
            act.activation(gtmp, learned, ACT.Exp, scale=-1.0).then_inc(g_e, 1)
            act.wait_ge(g_a, 1)
            act.activation(gtmp, gate, ACT.Exp, scale=-1.0).then_inc(g_e, 1)

        @block.vector
        def _(dve):
            for c in range(NC):
                dve.wait_ge(x_in[c], 16)
                for i in range(TPC):
                    dve.bn_stats(stats[:, c * TPC + i, :], x_sb[:, c * TPC + i, :]).then_inc(st_done, 1)
            dve.wait_ge(st_done, NT)
            for t in range(NT):
                dve.bn_aggr(mv[:, t, :], stats[:, t, :]).then_inc(st_done, 1)
            dve.wait_ge(rstd_done, 1)
            dve.wait_ge(w_in, 64)
            dve.wait_ge(primed, 1)

            def norm_chunk(c):
                for i in range(TPC):
                    t = c * TPC + i
                    dve.tensor_scalar(xn[:, i, :], x_sb[:, bass.ds(t, 1), :].rearrange("p a c -> p (a c)"),
                                      mv[:, bass.ds(t, 1), 0], rstd[:, bass.ds(t, 1)],
                                      ALU.subtract, ALU.mult).then_inc(xn_ready, 1)

            def split(c, g):
                own = c * 8 + 2 * g
                f, rest, part = qk_f32[:, g % 2, :], qk_rest[:, g % 2, :], qk_part[:, g % 2, :, :]
                dve.wait_ge(f_ready, c * 8 + (2 * (g + 1) + CREDIT[f_ready]))
                dve.tensor_tensor(rest, f, part[:, 0, :], ALU.subtract).then_inc(split_own, 1)
                dve.wait_ge(split_own, own + 1)
                dve.tensor_copy(part[:, 1, :], rest).then_inc(split_own, 1)
                dve.wait_ge(split_own, own + 2)
                dve.tensor_tensor(part[:, 2, :], rest, part[:, 1, :], ALU.subtract).then_inc(split_done, 1)

            def evacuate_v(c):
                for j in range(2):
                    dve.wait_ge(v_ready, c * 2 + (j + 1))
                    dve.tensor_tensor(v_rows[:, bass.ds(c * TPC + 2 * j, 2), :],
                                      ps[:, 4 + j, :].rearrange("p (a c) -> p a c", a=2), bv,
                                      ALU.add).then_inc(v_evac, 1)

            norm_chunk(0)
            with dve.Fori(0, NC - 1) as c:
                split(c, 0)
                split(c, 1)
                dve.wait_ge(t_ready, c + 1)
                norm_chunk(c + 1)
                split(c, 2)
                split(c, 3)
                evacuate_v(c)
            for g in range(4):
                split(NC - 1, g)
            evacuate_v(NC - 1)

            def combine_used(it):
                o = ps[:, 7, 0:P].rearrange("p (i e) -> p i e", i=TPC)
                dve.wait_ge(comb_ready, it + 1)
                dve.reciprocal(rinv[:, :], o[:, :, D]).then_inc(rinv_done, 1)
                dve.wait_ge(rinv_done, it + 1)
                dve.tensor_tensor(attn[:, bass.ds(it * (TPC * D), TPC * D)].rearrange("p (i d) -> p i d", i=TPC),
                                  o[:, :, 0:D], rinv[:, :].unsqueeze(2).to_broadcast([P, TPC, D]),
                                  ALU.mult).then_inc(comb_used, 1)

            def row_max(mi, it):
                dve.wait_ge(negmax_ready, mi + CREDIT[negmax_ready])
                for k in range(16):
                    dve.wait_ge(m_ready, mi * 16 + (k + 1))
                    dve.tensor_reduce(partial[:, k // 4, k % 4:k % 4 + 1], ps[:, 2 * (k % 2):2 * (k % 2) + 2, :], AX.XY,
                                      ALU.max).then_inc(max_used, 1)
                    if k == 3 and it is not None:
                        combine_used(it)
                dve.wait_ge(max_used, mi * 16 + (16 + CREDIT[max_used]))
                dve.wait_ge(nmparts_ready, mi + CREDIT[nmparts_ready])
                dve.tensor_reduce(negmax[:, :], partial[:, :, :], AX.X, ALU.max, negate=True).then_inc(negmax_ready, 1)

            with dve.Fori(0, AHEAD) as c:
                row_max(c, None)
            with dve.Fori(0, ITS - AHEAD) as it:
                row_max(it + AHEAD, it)
            with dve.Fori(ITS - AHEAD, ITS) as it:
                combine_used(it)
            combine_used(ITS)

            for n, (dst, src) in enumerate((
                (keysT.rearrange("p (a n) -> p a n", a=2), ps[:, 4:6, :]),
                (qpT, ps[:, 6, 0:2 * P].rearrange("p (k n) -> p k n", k=CC)),
                (routT, ps[:, 6, 2 * P:2 * P + RD]),
                (u1T, ps[:, 6, 3 * P:4 * P].rearrange("p (k n) -> p k n", k=CC)),
            )):
                if n == 0:
                    dve.wait_ge(w3_t, 1)
                dve.tensor_copy(dst, src).then_inc(w3_e, 1)
            dve.tensor_scalar(rkT[MASKROW:MASKROW + 1, :], rkT[MASKROW:MASKROW + 1, :], float(RD) ** 0.5, None,
                              ALU.mult).then_inc(w3_e, 1)
            dve.wait_ge(w3_t, 2)
            dve.tensor_copy(rkT[0:RD, :].rearrange("p (a n) -> p a n", a=2), ps[0:RD, 0:2, :]).then_inc(w3_e, 1)

            def tile_stats(src, n, own):
                dve.sem_inc(dve_passed, 1)
                for i in range(TPC):
                    last = dve.bn_stats(stats[:, i, :], src(i))
                last.then_inc(own, 1)
                dve.wait_ge(own, n + 1)
                dve.sem_inc(dve_passed, 1)
                for i in range(TPC):
                    last = dve.bn_aggr(mv[:, i, :], stats[:, i, :])
                return last

            def x_tile(c, i):
                return x_sb[:, bass.ds(c * TPC + i, 1), :].rearrange("p a c -> p (a c)")

            def h_tile(c, i):
                return v_rows[:, bass.ds(c * TPC + i, 1), :].rearrange("p a c -> p (a c)")

            def project_out(c):
                for j in range(2):
                    dve.wait_ge(y_psum, c * 2 + (j + 1 + CREDIT[y_psum]))
                    dve.tensor_tensor(y[:, 2 * j:2 * j + 2, :], ps[:, 2 + j, :].rearrange("p (a c) -> p a c", a=2),
                                      bproj, ALU.add).then_inc(y_evac, 1)
                dve.wait_ge(y_evac, c * 2 + (2 + CREDIT[y_evac]))
                tile_stats(lambda i: y[:, i, :], c * 7, y_own).then_inc(var_ready, 1)

            def add_block(c):
                dve.wait_ge(rs_ready, c * 2 + 1)
                for i in range(TPC):
                    last = dve.tensor_scalar(y[:, i, :], y[:, i, :], mv[:, i, 0:1], rstd[:, i:i + 1],
                                             ALU.subtract, ALU.mult)
                last.then_inc(y_own, 1)
                dve.wait_ge(y_own, c * 7 + 2)
                xc = x_sb[:, bass.ds(c * TPC, TPC), :]
                dve.tensor_tensor(xc, xc, y, ALU.add).then_inc(y_own, 1)

            def block_stats(c):
                dve.wait_ge(y_own, c * 7 + 3)
                tile_stats(lambda i: x_tile(c, i), c * 7 + 3, y_own).then_inc(var_ready, 1)

            def norm_block(c):
                dve.wait_ge(rs_ready, c * 2 + 2)
                for i in range(TPC):
                    last = dve.tensor_scalar(h_tile(c, i), x_tile(c, i), mv[:, i, 0:1], rstd[:, i:i + 1],
                                             ALU.subtract, ALU.mult)
                last.then_inc(h_ready, 1)

            def norm_stats(c):
                dve.wait_ge(h_ready, c + 1)
                tile_stats(lambda i: h_tile(c, i), c * 7 + 4, y_own).then_inc(y_own, 1)
                dve.wait_ge(y_own, c * 7 + 6)
                dve.tensor_copy(hvar[:, bass.ds(c * TPC, TPC)], mv[:, 0:TPC, 1]).then_inc(y_own, 1)
                dve.wait_ge(y_own, c * 7 + 7)

            def take_top(c, i):
                n = c * TPC + i
                sc = ps[:, sc_bank[i % 2]:sc_bank[i % 2] + 2, :]
                dve.wait_ge(sc_psum, n + 1)
                dve.sem_inc(dve_passed, 1)
                dve.max(top8[:, i, :], sc).then_inc(top_ready, 1)
                dve.wait_ge(top_ready, n + 1)
                dve.tensor_scalar(nbias[:, i:i + 1], top8[:, i, 0:1], -RSQ, None, ALU.mult)
                dve.match_replace(picked[i % 2], top8[:, i, :], sc, TAKEN).then_inc(picked_ready, 1)

            def weigh(c, i):
                n = c * TPC + i
                dve.wait_ge(e_ready, n + 1 + CREDIT[e_ready])
                dve.wait_ge(picked_ready, n + 1)
                dve.scalar_tensor_tensor(out=wts_flat[i % 2], in0=picked_flat[i % 2], scalar=TAKEN, in1=wts_flat[i % 2],
                                         op0=ALU.is_equal, op1=ALU.mult,
                                         accum_out=wsum[:, i:i + 1]).then_inc(w_sum, 1)
                dve.wait_ge(w_sum, n + 1)
                dve.reciprocal(wrec[:, i:i + 1], wsum[:, i:i + 1]).then_inc(wr_ready, 1)

            def keep_agg(c, i):
                n = c * TPC + i
                dve.wait_ge(agg_psum, n + 1 + CREDIT[agg_psum])
                dve.wait_ge(wr_ready, n + 1)
                dve.tensor_scalar(agg_tile(n), ps[:, 2 + i % 2, 0:C].rearrange("p (h d) -> p h d", h=H),
                                  wrec[:, i:i + 1], None, ALU.mult).then_inc(agg_ready, 1)

            def ffn_chunk(c, ahead):
                if ahead:
                    project_out(c + 1)
                take_top(c, 0)
                weigh(c, 0)
                dve.wait_ge(l_psum, c + 1)
                dve.tensor_copy(learned[:, bass.ds(c * TPC, TPC)], ps[:, 3, 0:TPC]).then_inc(l_ready, 1)
                take_top(c, 1)
                if ahead:
                    add_block(c + 1)
                weigh(c, 1)
                take_top(c, 2)
                keep_agg(c, 0)
                if ahead:
                    block_stats(c + 1)
                weigh(c, 2)
                take_top(c, 3)
                keep_agg(c, 1)
                if ahead:
                    norm_block(c + 1)
                weigh(c, 3)
                if ahead:
                    norm_stats(c + 1)
                keep_agg(c, 2)
                keep_agg(c, 3)

            project_out(0)
            add_block(0)
            block_stats(0)
            norm_block(0)
            norm_stats(0)
            with dve.Fori(0, NC - 1) as c:
                ffn_chunk(c, True)
            ffn_chunk(NC - 1, False)

            def step(sem_, n, ins):
                ins.then_inc(sem_, 1)
                dve.wait_ge(sem_, n)

            dve.wait_ge(lv_ready, 1)
            dve.reduce_sum(lvs, lv, axis=AX.X).then_inc(lv_own, 1)
            dve.tensor_scalar(learned, learned, u2b, None, ALU.add).then_inc(g_own, 1)
            dve.wait_ge(lvt_ready, 1)
            dve.tensor_scalar(lvm, ps[:, 2, 0:1], 1.0 / T, 1e-6, ALU.mult, ALU.add).then_inc(g_own, 1)
            dve.wait_ge(g_own, 2)
            dve.reciprocal(lvr, lvm).then_inc(g_own, 1)
            dve.wait_ge(g_own, 3)
            dve.tensor_scalar(lv, lv, lvr, 0.5, ALU.mult, ALU.mult).then_inc(g_own, 1)
            dve.wait_ge(g_e, 1)
            dve.tensor_scalar(gtmp, gtmp, 1.0, None, ALU.add).then_inc(g_own, 1)
            dve.wait_ge(g_own, 5)
            dve.reciprocal(gate, gtmp).then_inc(g_own, 1)
            dve.wait_ge(g_own, 6)
            dve.scalar_tensor_tensor(out=lv, in0=gate, scalar=2.5, in1=lv, op0=ALU.mult, op1=ALU.add).then_inc(g_own, 1)
            dve.wait_ge(g_own, 7)
            dve.tensor_scalar(lv, lv, 0.0, 5.0, ALU.max, ALU.min).then_inc(g_own, 1)
            dve.wait_ge(g_own, 8)
            dve.tensor_scalar(gate, lv, gw, gb, ALU.mult, ALU.add).then_inc(g_a, 1)
            dve.wait_ge(g_e, 2)
            dve.tensor_scalar(gtmp, gtmp, 1.0, None, ALU.add).then_inc(g_own, 1)
            dve.wait_ge(g_own, 9)
            dve.reciprocal(gate, gtmp).then_inc(g_own, 1)
            dve.wait_ge(g_own, 10)

            with dve.Fori(0, NC // 2) as c2:
                for b in range(2):
                    c = c2 * 2 + b
                    own = c2 * 6 + 3 * b
                    dve.wait_ge(res_ready, c2 * 2 + (b + CREDIT[res_ready]))
                    for i in range(TPC):
                        n = c * TPC + i
                        last = dve.scalar_tensor_tensor(
                            out=o2[:, i, :].rearrange("p (h d) -> p h d", h=H), in0=agg_tile(n),
                            scalar=gate[:, bass.ds(n, 1)], in1=h_tile(c, i).rearrange("p (h d) -> p h d", h=H),
                            op0=ALU.mult, op1=ALU.add)
                    last.then_inc(o_own, 1)
                    dve.wait_ge(o_own, own + 1)
                    tile_stats(lambda i: o2[:, i, :], own + 1, o_own).then_inc(o_var, 1)
                    dve.wait_ge(o_rs, c + 1)
                    for i in range(TPC):
                        last = dve.tensor_scalar(o2[:, i, :], o2[:, i, :], mv[:, i, 0:1], rstd[:, i:i + 1],
                                                 ALU.subtract, ALU.mult)
                    last.then_inc(o_own, 1)
                    dve.wait_ge(o_own, own + 3)
                    dve.wait_ge(out_done[b], c2 * 16 + 16)
                    dve.tensor_tensor(res[b], o2, x_sb[:, bass.ds(c * TPC, TPC), :], ALU.add).then_inc(res_ready, 1)

        @block.tensor
        def _(pe):
            def transpose_chunk(src, done):
                for i in range(TPC):
                    for k in range(CC):
                        last = pe.transpose(ps[:, k, P * i:P * (i + 1)], src[:, i, P * k:P * (k + 1)], ident[:, :])
                last.then_inc(done, 1)

            def project_qk(c):
                pe.wait_ge(xnT_ready, c + 1)
                for g in range(4):
                    pe.wait_ge(f_ready, c * 8 + 2 * (g + 1))
                    for k in range(CC):
                        last = pe.matmul(ps[:, 2 + g % 2, :], wqkv[:, k, P * g:P * (g + 1)], xnT[:, k, :],
                                         start=(k == 0), stop=(k == CC - 1))
                    last.then_inc(qk_ready, 1)

            def project_v(c):
                for j in range(2):
                    pe.wait_ge(v_evac, c * 2 + (j + 1))
                    for a in range(2):
                        i = 2 * j + a
                        for k in range(CC):
                            last = pe.matmul(ps[:, 4 + j, C * a:C * (a + 1)], xnT[:, k, P * i:P * (i + 1)],
                                             wqkv[:, k, 2 * C:3 * C], start=(k == 0), stop=(k == CC - 1))
                    last.then_inc(v_ready, 1)

            pe.wait_ge(primed, 1)
            pe.wait_ge(w_in, 64)
            pe.wait_ge(xn_ready, TPC)
            transpose_chunk(xn, t_ready)
            with pe.Fori(0, NC - 1) as c:
                project_qk(c)
                pe.wait_ge(xn_ready, c * TPC + 2 * TPC)
                transpose_chunk(xn, t_ready)
                project_v(c)
            project_qk(NC - 1)
            project_v(NC - 1)

            def max_pair(k, mi, b1, c):
                pe.wait_ge(max_used, mi * 16 + (k + 1))
                for e in range(2):
                    last = pe.matmul(ps[:, 2 * (k % 2) + e, :], q_stack[0:ROWS, b1, bass.ds(c * CH + (k // 4) * P, P)],
                                     k_stack[0:ROWS, b1, CH * (2 * (k % 4) + e):CH * (2 * (k % 4) + e + 1)],
                                     start=True, stop=True)
                last.then_inc(m_ready, 1)

            def score(g, i, it, b, c):
                pe.wait_ge(exp_done, it * NT + (4 * g + i + 1))
                pe.matmul(ps[:, 4 + i % 2, :], k_stack[0:ROWS + MROWS, b, P * (4 * g + i):P * (4 * g + i + 1)],
                          q_stack[0:ROWS + MROWS, b, bass.ds(c * CH, CH)], start=True, stop=True).then_inc(s_ready, 1)

            def weighted_values(g, it, b):
                pe.wait_ge(exp_done, it * NT + (4 * g + 4 + CREDIT[exp_done]))
                if g == 0:
                    pe.wait_ge(o_evac, it + 1)
                for j in range(4):
                    last = pe.matmul(ps[32 * j:32 * j + 32, 6, :], v_head[:, b, 4 * g + j, :], probs[:, g % 4, j, :],
                                     start=(g == 0), stop=(g == KG - 1))
                last.then_inc(pv_done, 1)

            def combine(it):
                pe.wait_ge(o_evac, it + 1)
                pe.wait_ge(comb_used, it + 1)
                for i in range(TPC):
                    last = pe.matmul(ps[:, 7, 32 * i:32 * i + D + 1], o_sb[:, P * i:P * (i + 1)], sel[:, :],
                                     start=True, stop=True)
                last.then_inc(comb_ready, 1)

            def max_row(n):
                pe.wait_ge(nmparts_ready, n + 1 + CREDIT[nmparts_ready])
                pe.wait_ge(comb_used, n + CREDIT[comb_used])
                for i in range(TPC):
                    last = pe.matmul(ps[0:MROWS, 7, P * i:P * (i + 1)], nm_parts[:, i, :], ident_bf[:, :],
                                     start=True, stop=True)
                last.then_inc(mrow_ready, 1)

            def first_scores(it, b, c):
                pe.wait_ge(mrow_done, it + 1)
                score(0, 0, it, b, c)
                score(0, 1, it, b, c)

            def attend(it, b, c, ahead, following):
                for g in range(KG):
                    if g:
                        score(g, 0, it, b, c)
                        score(g, 1, it, b, c)
                        weighted_values(g - 1, it, b)
                    score(g, 2, it, b, c)
                    score(g, 3, it, b, c)
                    for k in (2 * g, 2 * g + 1):
                        if ahead:
                            max_pair(k, it + AHEAD, *ahead)
                    if g == 1:
                        combine(it)
                    if g == 4 and following:
                        max_row(it + 1)
                if following:
                    first_scores(it + 1, *following)
                weighted_values(KG - 1, it, b)

            pe.wait_ge(stack_in[0], 16 * 12)
            with pe.Fori(0, AHEAD) as c:
                for k in range(16):
                    max_pair(k, c, 0, c)
            max_row(0)
            first_scores(0, 0, 0)
            with pe.Fori(0, H // NB) as r:
                for b in range(NB):
                    first = (r * NB + b) * NC
                    b1 = (b + 1) % NB
                    pe.wait_ge(vhead_ready, r * NB + (b + 1))
                    pe.sem_inc(pe_passed, 1)
                    with pe.Fori(0, NC - AHEAD) as c:
                        attend(first + c, b, c, (b, c + AHEAD), (b, c + 1))
                    pe.wait_ge(stack_in[b1], (r + 1 + (b + 1) // NB) * (16 * 12))
                    for c in range(NC - AHEAD, NC):
                        attend(first + c, b, c, (b1, c + AHEAD - NC), (b, c + 1) if c + 1 < NC else (b1, 0))
            first = (H - 1) * NC
            pe.wait_ge(vhead_ready, H)
            with pe.Fori(0, NC - AHEAD) as c:
                attend(c + first, 0, c, (0, c + AHEAD), (0, c + 1))
            attend(first + NC - 2, 0, NC - 2, None, (0, NC - 1))
            attend(first + NC - 1, 0, NC - 1, None, None)
            combine(ITS)

            pe.wait_ge(w3_in, 16 * W3_LOADS)
            pe.wait_ge(w3_init, 4)
            for v in range(NV):
                pe.transpose(ps[:, 4 + v // 4, P * (v % 4):P * (v % 4 + 1)], keys[:, v, :], ident[:, :])
            for k in range(CC):
                pe.transpose(ps[:, 6, P * k:P * (k + 1)], qpw[:, P * k:P * (k + 1)], ident[:, :])
                pe.transpose(ps[:, 6, 3 * P + F1 * k:3 * P + F1 * (k + 1)], u1w[0:F1, P * k:P * (k + 1)], ident[0:F1, 0:F1])
            pe.transpose(ps[:, 6, 2 * P:2 * P + RD], routw[0:RD, :], ident[0:RD, 0:RD]).then_inc(w3_t, 1)
            pe.wait_ge(w3_e, 4)
            for a in range(2):
                last = pe.matmul(ps[0:RD, a, :], routT, keysT[:, CH * a:CH * (a + 1)], start=True, stop=True)
            last.then_inc(w3_t, 1)
            pe.wait_ge(w3_e, 6)
            def attn_transpose(c):
                pe.wait_ge(stage_a_ready, c + 1)
                transpose_chunk(stage_a, aT_psum)

            def project_out(c, j):
                pe.wait_ge(aT_ready, c + 1)
                pe.wait_ge(y_evac, c * 2 + (j + 1))
                for a in range(2):
                    i = 2 * j + a
                    for k in range(CC):
                        last = pe.matmul(ps[:, 2 + j, C * a:C * (a + 1)], aT[:, k, P * i:P * (i + 1)], wproj[:, k, :],
                                         start=(k == 0), stop=(k == CC - 1))
                last.then_inc(y_psum, 1)

            def lookup_scores(c, i):
                n = c * TPC + i
                pe.wait_ge(e_ready, n - 1 + CREDIT[e_ready])
                for a in range(2):
                    last = pe.matmul(ps[:, sc_bank[i % 2] + a, :], rqT[0:MASKROW + 1, P * i:P * (i + 1)],
                                     rkT[0:MASKROW + 1, CH * a:CH * (a + 1)], start=True, stop=True)
                last.then_inc(sc_psum, 1)

            def ffn_chunk(c, one_ahead, two_ahead):
                pe.wait_ge(wT_ready, c * TPC + CREDIT[wT_ready])
                pe.wait_ge(stage_h_ready, c + 1)
                transpose_chunk(stage_h, hT_psum)
                pe.wait_ge(agg_ready, c * TPC + CREDIT[agg_ready])
                if one_ahead:
                    project_out(c + 1, 0)
                pe.wait_ge(hT_ready, c + 1)
                pe.wait_ge(e_ready, c * TPC + CREDIT[e_ready])
                for k in range(CC):
                    last = pe.matmul(ps[:, 4, :], qpT[:, k, :], hT[:, k, :], start=(k == 0), stop=(k == CC - 1))
                last.then_inc(qy_psum, 1)
                for k in range(CC):
                    last = pe.matmul(ps[0:F1, 7, :], u1T[:, k, :], hT[:, k, :], start=(k == 0), stop=(k == CC - 1))
                last.then_inc(u_psum, 1)
                pe.wait_ge(qy_ready, c + 1)
                pe.matmul(ps[0:RD, 6, :], routT, queryT, start=True, stop=True).then_inc(rq_psum, 1)
                if one_ahead:
                    project_out(c + 1, 1)
                pe.wait_ge(rq_ready, c + 1)
                lookup_scores(c, 0)
                pe.wait_ge(u_ready, c + 1)
                lookup_scores(c, 1)
                if one_ahead:
                    pe.wait_ge(y_evac, c * 2 + (4 + CREDIT[y_evac]))
                for i in range(TPC):
                    last = pe.matmul(ps[:, 3, i:i + 1], g1T[0:F1, P * i:P * (i + 1)], u2w[0:F1, :], start=True, stop=True)
                last.then_inc(l_psum, 1)
                if two_ahead:
                    attn_transpose(c + 2)
                    pe.wait_ge(aT_ready, c + 3)
                for i in range(TPC):
                    n = c * TPC + i
                    pe.wait_ge(wr_ready, n + 1)
                    pe.wait_ge(wT_ready, n + CREDIT[wT_ready])
                    for v in range(NV):
                        last = pe.transpose(ps[:, v // 4, P * (v % 4):P * (v % 4 + 1)],
                                            wts_flat[i % 2][:, P * v:P * (v + 1)], ident[:, :])
                    last.then_inc(wT_psum, 1)
                    if i + 2 < TPC:
                        lookup_scores(c, i + 2)
                    pe.wait_ge(wT_ready, n + 1 + CREDIT[wT_ready])
                    if i == 1:
                        pe.wait_ge(l_ready, c + 1 + CREDIT[l_ready])
                    if i >= 2:
                        pe.wait_ge(agg_ready, n - 1 + CREDIT[agg_ready])
                    for v in range(NV):
                        last = pe.matmul(ps[:, 2 + i % 2, 0:C], wT[:, v, :], values[:, v, :],
                                         start=(v == 0), stop=(v == NV - 1))
                    last.then_inc(agg_psum, 1)

            attn_transpose(0)
            project_out(0, 0)
            project_out(0, 1)
            attn_transpose(1)
            pe.wait_ge(aT_ready, 2)
            with pe.Fori(0, NC - 2) as c:
                ffn_chunk(c, True, True)
            ffn_chunk(NC - 2, True, False)
            ffn_chunk(NC - 1, False, False)
            pe.wait_ge(lv_own, 1)
            pe.wait_ge(agg_ready, NT + CREDIT[agg_ready])
            pe.matmul(ps[:, 2, 0:1], ones, lvs, start=True, stop=True).then_inc(lvt_ready, 1)


INPUTS = ["L0_attn_x", "L0_attn_w_qkv", "L0_attn_b_qkv", "L0_attn_w_proj", "L0_attn_b_proj", "L0_ffn_q_proj_w",
          "L0_ffn_router_w", "L0_ffn_aux_keys", "L0_ffn_aux_values", "L0_ffn_reliability_mask", "L0_ffn_unc_w1",
          "L0_ffn_unc_b1", "L0_ffn_unc_w2", "L0_ffn_unc_b2", "L0_ffn_gate_w1", "L0_ffn_gate_bias"]


def kernel(**inputs):
    import numpy as np
    import concourse.bacc as bacc
    from concourse.bass_utils import run_bass_kernel_spmd

    nc = bacc.Bacc("TRN2", target_bir_lowering=False, num_devices=1)
    arrays, args = {}, []
    for name in INPUTS:
        a = np.ascontiguousarray(inputs[name])
        arrays[name] = a
        args.append(nc.dram_tensor(name, a.shape, mybir.dt.from_np(a.dtype), kind="ExternalInput").ap())
    shape = arrays["L0_attn_x"].shape
    args.append(nc.dram_tensor("out", shape, F32, kind="ExternalOutput").ap())
    sandwich_kernel(nc, *args)
    result = run_bass_kernel_spmd(nc, [arrays], core_ids=[0])
    return result.results[0]["out"]
```

```python
from contextlib import ExitStack

import concourse.bass as bass
from concourse import mybir

F32 = mybir.dt.float32
BF16 = mybir.dt.bfloat16
ALU = mybir.AluOpType
ACT = mybir.ActivationFunctionType
AX = mybir.AxisListType

P = 128
CH = 512
EPS = 1e-5
NB = 3
SLOT_Q = [0, 0, 1, 0, 1, 2]
SLOT_K = [0, 1, 0, 2, 1, 0]
TAKEN = -3.0e38


def sandwich_kernel(nc, x, w_qkv, b_qkv, w_proj, b_proj, q_proj_w, router_w, aux_keys, aux_values,
                    reliability_mask, unc_w1, unc_b1, unc_w2, unc_b2, gate_w1, gate_bias, out):
    _, T, C = x.shape
    H = 16
    D = C // H
    NT = T // P
    NC = T // CH
    TPC = CH // P
    CC = C // P
    BOT = q_proj_w.shape[0]
    RD = router_w.shape[0]
    N = aux_keys.shape[0]
    NV = N // P
    F1 = unc_w1.shape[0]
    SCALE = float(D) ** -0.5
    RSQ = float(RD) ** -0.5
    ROWS = 6 * D
    MROWS = 3
    KG = NT // 2
    AHEAD = 2
    PAIRS = NC // 2
    ITS = H * PAIRS
    LEAD = 6
    W3_LOADS = 14
    MASKROW = 64
    assert ROWS == 96 and C == 256 and T == 4096 and BOT == P and RD <= MASKROW and N == 1024

    x_t = x[0].rearrange("(t p) c -> p t c", p=P)
    out_t = out[0].rearrange("(t p) c -> p t c", p=P)
    parts_dram = nc.dram_tensor("qk_parts", (2, 3, C, T), BF16, kind="Internal").ap()

    with ExitStack() as ctx:
        def sb(name, shape, dt=F32):
            return ctx.enter_context(nc.sbuf_tensor(name, shape, dt))

        def sem(name):
            return ctx.enter_context(nc.semaphore(name))

        ps = ctx.enter_context(nc.psum_tensor("ps", [P, 8, CH], F32))

        x_sb = sb("x_sb", [P, NT, C])
        v_all = sb("v_all", [P, NT * C])
        attn = sb("attn", [P, NC * TPC * C + 8 * D])
        work = sb("work", [P, 8192])
        q_raw = sb("q_raw", [P, NB * T // 2])
        k_raw = sb("k_raw", [P, NB * T // 2])
        v_head = sb("v_head", [P, NB, NT, 32])
        o_sb = sb("o_sb", [P, CH])
        ident = sb("ident", [P, P])
        ident_bf = sb("ident_bf", [P, P], BF16)
        sel = sb("sel", [P, 2 * (D + 1)])
        stats = sb("stats", [P, TPC, 6])
        mv = sb("mv", [P, TPC, 2])
        rstd = sb("rstd", [P, TPC])
        veps = sb("veps", [P, TPC])
        hvar = sb("hvar", [P, NT])
        minus_half = sb("minus_half", [P, TPC])
        partial = sb("partial", [P, TPC, 4])
        negmax = sb("negmax", [P, TPC])
        nm_rest = sb("nm_rest", [P, 2, TPC])
        nm_parts = sb("nm_parts", [P, TPC, MROWS], BF16)
        rinv = sb("rinv", [P, TPC, 2])
        lead = sb("lead", [P, 1])

        q_stack = q_raw[:, :].bitcast(BF16).rearrange("p (b t) -> p b t", b=NB)
        k_stack = k_raw[:, :].bitcast(BF16).rearrange("p (b t) -> p b t", b=NB)
        v_rows = v_all[:, :].rearrange("p (t c) -> p t c", c=C)

        xn = work[:, 0:1024].rearrange("p (t c) -> p t c", t=TPC)
        wqkv = work[:, 2048:3584].rearrange("p (k n) -> p k n", k=CC)
        qk_f32 = k_raw[:, 0:4 * CH].rearrange("p (g t) -> p g t", g=4)
        qk_rest = k_raw[:, 4 * CH:8 * CH].rearrange("p (g t) -> p g t", g=4)
        qk_part = q_raw[:, 0:6 * CH].bitcast(BF16).rearrange("p (g r t) -> p g r t", g=4, r=3)
        bv = work[:, 3584:4096].rearrange("p (a c) -> p a c", a=2)
        bqk = work[:, 4096:4100]
        xnT = attn[:, 0:NC * CC * CH].rearrange("p (c k t) -> p c k t", c=NC, k=CC)
        v_src = [work[:, 1024 * b:1024 * (b + 1)].rearrange("p (k t) -> p k t", k=CC) for b in range(2)]
        probs = work[:, :].rearrange("p (r j t) -> p r j t", r=4, j=4)
        v_head_flat = v_head[:, :, :, :].rearrange("p b t d -> p (b t d)")
        stage_a = v_head_flat[:, 1024:2048].rearrange("p (t c) -> p t c", t=TPC)
        aT = v_head_flat[:, 2048:3072].rearrange("p (k t) -> p k t", k=CC)
        stage_h = work[:, 3072:4096].rearrange("p (t c) -> p t c", t=TPC)
        hT = work[:, 4096:5120].rearrange("p (k t) -> p k t", k=CC)
        queryT = work[:, 5120:5632]
        rqT = work[:, 5632:6144]
        g1T = work[:, 6144:6656]
        o2 = [work[:, 1024 * b:1024 * (b + 1)].rearrange("p (t c) -> p t c", t=TPC) for b in range(4)]
        res = [work[:, 1024 * (b + 4):1024 * (b + 5)].rearrange("p (t c) -> p t c", t=TPC) for b in range(2)]
        picked_flat = [q_raw[:, 1024 * (b + 2):1024 * (b + 3)] for b in range(2)]
        wts_flat = [k_raw[:, 1024 * b:1024 * (b + 1)] for b in range(2)]
        picked = [v.rearrange("p (a n) -> p a n", a=2) for v in picked_flat]
        wts = [v.rearrange("p (a n) -> p a n", a=2) for v in wts_flat]
        sc_bank = [4, 6]
        values = k_raw[:, 2048:4096].rearrange("p (v c) -> p v c", v=NV)
        rkT = k_raw[:, 4096:5120]
        wproj = k_raw[:, 5120:5632].rearrange("p (k n) -> p k n", k=CC)
        bproj = k_raw[:, 5632:6144].rearrange("p (a c) -> p a c", a=2)
        keys = q_raw[:, 2048:3072].rearrange("p (v c) -> p v c", v=NV)
        keysT = q_raw[:, 3072:4096]
        qpw = q_raw[:, 4096:4352]
        qpT = q_raw[:, 4352:4608].rearrange("p (k n) -> p k n", k=CC)
        routw = q_raw[:, 4608:4736]
        routT = q_raw[:, 4736:4736 + RD]
        u1w = q_raw[:, 4800:5056]
        u1T = q_raw[:, 5056:5184].rearrange("p (k n) -> p k n", k=CC)
        ones = q_raw[:, 5184:5312]
        small = q_raw[:, 5312:5376]
        u1b, u2w, u2b, gw, gb = (small[:, i:i + 1] for i in range(5))
        lvs, lvm, lvr = (small[:, i:i + 1] for i in range(5, 8))
        nbias, wsum, wrec = (small[:, i:i + TPC] for i in range(8, 8 + 3 * TPC, TPC))
        lv, learned, gate, gtmp = (q_raw[:, i:i + NT] for i in range(5376, 5376 + 4 * NT, NT))
        top8 = q_raw[:, 5504:5536].rearrange("p (i e) -> p i e", i=TPC)
        o_mv = q_raw[:, 5536:5568].rearrange("p (b t s) -> p b t s", b=4, s=2)
        o_rstd, o_nmean, o_shift = (q_raw[:, i:i + 16].rearrange("p (b t) -> p b t", b=4) for i in range(5568, 5616, 16))
        wT = q_raw[:, 0:1024].rearrange("p (v t) -> p v t", v=NV)
        wT2 = q_raw[:, 0:1024].rearrange("p (a n) -> p a n", a=2)

        attn_h = attn[:, 8 * D:].rearrange("p (h t d) -> p h t d", h=H, t=NT)

        def agg_tile(n):
            return attn_h[:, :, bass.ds(n, 1), :].rearrange("p h a d -> p (h a) d")

        x_in = [sem(f"x_in{c}") for c in range(3)]
        wqkv_in = sem("wqkv_in")
        w_in = sem("w_in")
        primed = sem("primed")
        consts = sem("consts")
        st_own = sem("st_own")
        st_done = sem("st_done")
        rstd_own = sem("rstd_own")
        rstd_done = sem("rstd_done")
        pool_own = sem("pool_own")
        xn_ready = sem("xn_ready")
        t_ready = sem("t_ready")
        xnT_ready = sem("xnT_ready")
        qk_ready = sem("qk_ready")
        f_ready = sem("f_ready")
        split_own = sem("split_own")
        two_parts = sem("two_parts")
        split_done = sem("split_done")
        parts_out = [sem(f"parts_out{g}") for g in range(4)]
        vsrc_ready = sem("vsrc_ready")
        v_ready = sem("v_ready")
        v_evac = sem("v_evac")
        v_biased = sem("v_biased")
        stack_in = [sem(f"stack_in{b}") for b in range(NB)]
        s_ready = sem("s_ready")
        exp_done = sem("exp_done")
        m_ready = sem("m_ready")
        max_used = sem("max_used")
        negmax_ready = sem("negmax_ready")
        nmparts_ready = sem("nmparts_ready")
        vhead_ready = sem("vhead_ready")
        pv_done = sem("pv_done")
        o_evac = sem("o_evac")
        comb_ready = sem("comb_ready")
        rinv_done = sem("rinv_done")
        comb_used = sem("comb_used")
        mrow_ready = sem("mrow_ready")
        mrow_done = sem("mrow_done")
        dve_passed = sem("dve_passed")
        pool_passed = sem("pool_passed")
        pe_passed = sem("pe_passed")
        w3_in = sem("w3_in")
        w3_init = sem("w3_init")
        w3_t = sem("w3_t")
        w3_e = sem("w3_e")
        pow_own = sem("pow_own")
        stage_a_ready = sem("stage_a_ready")
        stage_h_ready = sem("stage_h_ready")
        aT_psum = sem("aT_psum")
        aT_ready = sem("aT_ready")
        y_psum = sem("y_psum")
        y_own = sem("y_own")
        y_evac = sem("y_evac")
        var_ready = sem("var_ready")
        rs_ready = sem("rs_ready")
        h_ready = sem("h_ready")
        hT_psum = sem("hT_psum")
        hT_ready = sem("hT_ready")
        qy_psum = sem("qy_psum")
        qy_ready = sem("qy_ready")
        rq_psum = sem("rq_psum")
        rq_ready = sem("rq_ready")
        u_psum = sem("u_psum")
        u_ready = sem("u_ready")
        l_psum = sem("l_psum")
        l_ready = sem("l_ready")
        sc_psum = sem("sc_psum")
        top_ready = sem("top_ready")
        picked_ready = sem("picked_ready")
        e_ready = sem("e_ready")
        w_sum = sem("w_sum")
        wr_ready = sem("wr_ready")
        wT_psum = sem("wT_psum")
        wT_ready = sem("wT_ready")
        agg_psum = sem("agg_psum")
        agg_ready = sem("agg_ready")
        lv_ready = sem("lv_ready")
        lv_own = sem("lv_own")
        lvt_ready = sem("lvt_ready")
        g_own = sem("g_own")
        g_e = sem("g_e")
        g_a = sem("g_a")
        o_own = sem("o_own")
        o_var = sem("o_var")
        o_rs = sem("o_rs")
        o_pow = sem("o_pow")
        z_ready = sem("z_ready")
        res_ready = sem("res_ready")
        out_done = [sem("out_done0"), sem("out_done1")]

        CREDIT = {exp_done: 2, max_used: 2, pv_done: 4, o_evac: 1, comb_used: 1, nmparts_ready: 1, negmax_ready: 1,
                  res_ready: 4, mrow_ready: 1, mrow_done: 1, y_psum: 1,
                  f_ready: 8, split_done: 4, v_evac: 2, v_ready: 4, aT_psum: 1, hT_psum: 1, y_evac: 2, e_ready: 2, wT_ready: 1,
                  agg_ready: 2, l_ready: 1, agg_psum: 1,
                  wT_psum: 2}

        block = ctx.enter_context(nc.Block())

        @block.sync
        def _(sp):
            for c in range(NC):
                sp.dma_start(x_sb[:, TPC * c:TPC * (c + 1), :], x_t[:, TPC * c:TPC * (c + 1), :]).then_inc(x_in[min(c, 2)], 16)
            with sp.Fori(0, NC) as c:
                for g in range(4):
                    sp.wait_ge(split_done, c * 4 + (g + 1 + CREDIT[split_done]))
                    dst = parts_dram[g // 2, :, (g % 2) * P:(g % 2 + 1) * P, bass.ds(c * CH, CH)]
                    sp.dma_start(dst.rearrange("r f t -> f r t"), qk_part[:, g, :, :]).then_inc(parts_out[g], 16)
            for g in range(4):
                sp.wait_ge(parts_out[g], 16 * (NC + 1))

            def load_stack(h, b):
                for s in range(6):
                    for stack, qk, part in ((k_stack, 1, SLOT_K[s]), (q_stack, 0, SLOT_Q[s])):
                        sp.dma_start(stack[D * s:D * (s + 1), b, 0:T], parts_dram[qk, part, bass.ds(h * D, D), :]
                                     ).then_inc(stack_in[b], 16)

            for b in range(NB):
                load_stack(b, b)
            with sp.Fori(1, H // NB) as r:
                for b in range(NB):
                    sp.wait_ge(pv_done, r * (NB * PAIRS * KG) + ((b - 2) * PAIRS * KG + CREDIT[pv_done]))
                    load_stack(r * NB + b, b)
            sp.wait_ge(pv_done, (H - 3) * PAIRS * KG + CREDIT[pv_done])
            load_stack(H - 1, (H - 1) % NB)

            sp.wait_ge(pv_done, (ITS - PAIRS) * KG + CREDIT[pv_done])
            sp.wait_ge(w3_init, 2)
            for dst, src in (
                (wproj, w_proj.rearrange("(k p) n -> p k n", p=P)),
                (bproj[:, 0, :], b_proj.partition_broadcast(P)),
                (bproj[:, 1, :], b_proj.partition_broadcast(P)),
                (keys, aux_keys.rearrange("(v p) d -> p v d", p=P)),
                (qpw, q_proj_w),
                (routw[0:RD, :], router_w),
                (u1w[0:F1, :], unc_w1),
                (u1b[0:F1, :], unc_b1.rearrange("(f a) -> f a", a=1)),
                (u2w[0:F1, :], unc_w2.rearrange("a f -> f a")),
                (u2b, unc_b2.partition_broadcast(P)),
                (gw, gate_w1.partition_broadcast(P)),
                (gb, gate_bias.partition_broadcast(P)),
                (rkT[MASKROW:MASKROW + 1, :], reliability_mask.rearrange("(a n) -> a n", a=1)),
                (values, aux_values.rearrange("(v p) d -> p v d", p=P)),
            ):
                sp.dma_start(dst, src, allow_slow_non_contiguous=True).then_inc(w3_in, 16)

            with sp.Fori(0, NC // 2) as c2:
                for b in range(2):
                    sp.wait_ge(res_ready, c2 * 2 + (b + 1 + CREDIT[res_ready]))
                    sp.dma_start(out_t[:, bass.ds(c2 * (2 * TPC) + b * TPC, TPC), :], res[b]).then_inc(out_done[b], 16)
            for b in range(2):
                sp.wait_ge(out_done[b], 16 * (NC // 2 + 1))

        @block.gpsimd
        def _(pool):
            pool.dma_start(wqkv, w_qkv.rearrange("(k p) n -> p k n", p=P)).then_inc(wqkv_in, 16)
            pool.dma_start(bqk, b_qkv[0:2 * C].rearrange("(g p) -> p g", p=P), allow_slow_non_contiguous=True).then_inc(w_in, 16)
            for a in range(2):
                pool.dma_start(bv[:, a, :], b_qkv[2 * C:3 * C].partition_broadcast(P)).then_inc(w_in, 16)
            pool.memset(minus_half[:], -0.5).then_inc(consts, 1)
            pool.memset(ident[:], 0.0).then_inc(consts, 1)
            pool.wait_ge(consts, 2)
            pool.affine_select(out=ident[:], in_=ident[:], compare_op=ALU.not_equal, fill=1.0, base=0,
                               pattern=[[-1, P]], channel_multiplier=1).then_inc(consts, 1)
            pool.wait_ge(consts, 3)
            pool.tensor_copy(ident_bf[:], ident[:]).then_inc(consts, 1)
            pool.wait_ge(consts, 4)
            for s, n in CREDIT.items():
                if n:
                    pool.sem_inc(s, n)
            for s in parts_out + out_done:
                pool.sem_inc(s, 16)
            pool.sem_inc(primed, 1)

            def powers(n, own, rs):
                pool.sem_inc(pool_passed, 1)
                pool.tensor_scalar(veps[:, 0:TPC], mv[:, 0:TPC, 1], EPS, None, ALU.add).then_inc(own, 1)
                pool.wait_ge(own, n)
                pool.tensor_tensor(rstd[:, 0:TPC], veps[:, 0:TPC], minus_half[:, 0:TPC], ALU.pow).then_inc(rs, 1)

            def x_powers(c):
                pool.wait_ge(st_done, c + 1)
                powers(c + 1, rstd_own, rstd_done)

            def third_part(c, g):
                pool.wait_ge(two_parts, c * 4 + (g + 1))
                pool.tensor_tensor(qk_part[:, g, 2, :], qk_rest[:, g, :], qk_part[:, g, 1, :],
                                   ALU.subtract).then_inc(split_done, 1)

            x_powers(0)
            x_powers(1)
            with pool.Fori(0, NC - 2) as c:
                third_part(c, 0)
                third_part(c, 1)
                x_powers(c + 2)
                third_part(c, 2)
                third_part(c, 3)
            with pool.Fori(NC - 2, NC) as c:
                for g in range(4):
                    third_part(c, g)

            pool.memset(sel[:], 0.0).then_inc(consts, 1)
            pool.memset(o_sb[:], 1.0).then_inc(consts, 1)
            pool.memset(v_head[:], 0.0).then_inc(consts, 1)
            pool.wait_ge(consts, 7)
            pool.memset(k_stack[ROWS:ROWS + MROWS, :, :], 1.0).then_inc(consts, 1)
            pool.wait_ge(consts, 8)
            pool.memset(v_head[:, :, :, D], 1.0).then_inc(consts, 1)
            pool.wait_ge(consts, 9)
            for j in range(4):
                half = sel[:, (j // 2) * (D + 1):(j // 2 + 1) * (D + 1)]
                pool.affine_select(out=half, in_=half, compare_op=ALU.not_equal, fill=1.0, base=-32 * j,
                                   pattern=[[-1, D + 1]], channel_multiplier=1).then_inc(consts, 1)
                pool.wait_ge(consts, 10 + j)

            def copy_v(h, b):
                pool.tensor_copy(v_head[:, b, :, 0:D], v_rows[:, :, bass.ds(h * D, D)]).then_inc(vhead_ready, 1)

            with pool.Fori(0, NC) as c:
                for j in range(2):
                    pool.wait_ge(v_evac, c * 2 + (j + 1 + CREDIT[v_evac]))
                    pair = v_rows[:, bass.ds(c * TPC + 2 * j, 2), :]
                    pool.tensor_tensor(pair, pair, bv, ALU.add).then_inc(v_biased, 1)
            pool.wait_ge(v_biased, 2 * NC)
            copy_v(0, 0)

            def split_max(mi):
                pool.wait_ge(negmax_ready, mi + 1 + CREDIT[negmax_ready])
                pool.wait_ge(mrow_ready, mi + CREDIT[mrow_ready])
                pool.sem_inc(pool_passed, 1)
                pool.tensor_copy(nm_parts[:, :, 0], negmax[:, :]).then_inc(pool_own, 1)
                pool.wait_ge(pool_own, mi * 4 + 1)
                pool.tensor_tensor(nm_rest[:, 0, :], negmax[:, :], nm_parts[:, :, 0], ALU.subtract).then_inc(pool_own, 1)
                pool.wait_ge(pool_own, mi * 4 + 2)
                pool.sem_inc(pool_passed, 1)
                pool.tensor_copy(nm_parts[:, :, 1], nm_rest[:, 0, :]).then_inc(pool_own, 1)
                pool.wait_ge(pool_own, mi * 4 + 3)
                pool.tensor_tensor(nm_rest[:, 1, :], nm_rest[:, 0, :], nm_parts[:, :, 1], ALU.subtract).then_inc(pool_own, 1)
                pool.wait_ge(pool_own, mi * 4 + 4)
                pool.sem_inc(pool_passed, 1)
                pool.tensor_copy(nm_parts[:, :, 2], nm_rest[:, 1, :]).then_inc(nmparts_ready, 1)

            with pool.Fori(0, AHEAD) as c:
                split_max(c)
            with pool.Fori(0, H // NB) as r:
                for b in range(NB):
                    pool.wait_ge(pv_done, r * (NB * PAIRS * KG) + (b * PAIRS * KG + CREDIT[pv_done]))
                    pool.sem_inc(pool_passed, 1)
                    copy_v(r * NB + (b + 1), (b + 1) % NB)
                    with pool.Fori(0, NC) as c:
                        split_max(r * (NB * NC) + c + (b * NC + AHEAD))
            pool.wait_ge(pv_done, (ITS - PAIRS) * KG + CREDIT[pv_done])
            pool.memset(rkT, 0.0).then_inc(w3_init, 1)
            pool.memset(ones, 1.0).then_inc(w3_init, 1)
            with pool.Fori(H * NC - NC + AHEAD, H * NC) as c:
                split_max(c)

            def stage_attn(c):
                pool.wait_ge(aT_psum, c + CREDIT[aT_psum])
                pool.sem_inc(pool_passed, 1)
                for i in range(TPC):
                    last = pool.tensor_copy(stage_a[:, i, :].rearrange("p (h d) -> p h d", h=H),
                                            attn_h[:, :, bass.ds(c * TPC + i, 1), :].rearrange("p h a d -> p (h a) d"))
                last.then_inc(stage_a_ready, 1)

            def block_powers(c):
                for k in range(2):
                    pool.wait_ge(var_ready, c * 2 + (k + 1))
                    powers(c * 2 + (k + 1), pow_own, rs_ready)

            pool.wait_ge(comb_used, ITS - PAIRS + 2 + CREDIT[comb_used])
            stage_attn(0)
            stage_attn(1)
            block_powers(0)
            pool.wait_ge(comb_used, ITS + 1 + CREDIT[comb_used])
            pool.memset(rqT, 0.0).then_inc(w3_init, 1)
            pool.wait_ge(w3_init, 3)
            pool.memset(rqT[MASKROW:MASKROW + 1, :], 1.0).then_inc(w3_init, 1)
            pool.wait_ge(w3_init, 4)
            stage_attn(2)
            with pool.Fori(1, NC - 2) as c:
                block_powers(c)
                stage_attn(c + 2)
            for c in range(NC - 2, NC):
                block_powers(c)

            def result_powers(c, b):
                pool.wait_ge(o_var, c + 1)
                pool.sem_inc(pool_passed, 1)
                pool.tensor_scalar(veps[:, :], o_mv[:, b, :, 1], EPS, None, ALU.add).then_inc(o_pow, 1)
                pool.wait_ge(o_pow, c * 2 + 1)
                pool.tensor_tensor(o_rstd[:, b, :], veps[:, :], minus_half[:, :], ALU.pow).then_inc(o_pow, 1)
                pool.wait_ge(o_pow, c * 2 + 2)
                pool.tensor_tensor(o_shift[:, b, :], o_nmean[:, b, :], o_rstd[:, b, :], ALU.mult).then_inc(o_rs, 1)

            def add_result(c, b, out_count):
                pool.wait_ge(z_ready, c + 1)
                pool.wait_ge(out_done[b % 2], out_count)
                pool.sem_inc(pool_passed, 1)
                pool.tensor_tensor(res[b % 2], o2[b], x_sb[:, bass.ds(c * TPC, TPC), :], ALU.add).then_inc(res_ready, 1)

            result_powers(0, 0)
            with pool.Fori(0, NC // 4 - 1) as c4:
                for b in range(4):
                    result_powers(c4 * 4 + (b + 1), (b + 1) % 4)
                    add_result(c4 * 4 + b, b, c4 * 32 + 16 * (b // 2 + 1))
            for b in range(4):
                c = NC - 4 + b
                if b < 3:
                    result_powers(c + 1, b + 1)
                add_result(c, b, 16 * (c // 2 + 1))

        @block.scalar
        def _(act):
            act.wait_ge(primed, 1)
            act.activation(lead[:, :], ident[:, 0:1], ACT.Copy)

            def move_xnT(c):
                act.wait_ge(t_ready, c + 1)
                act.activation(xnT[:, bass.ds(c, 1), :, :].rearrange("p a k t -> p (a k) t"), ps[:, 0:2, :],
                               ACT.Copy).then_inc(xnT_ready, 1)

            def evacuate_qk(c, g):
                act.wait_ge(qk_ready, c * 4 + (g + 1))
                act.wait_ge(split_done, c * 4 + (g + 1))
                act.wait_ge(parts_out[g], c * 16 + 16)
                act.activation(qk_f32[:, g, :], ps[:, 2 + g, :], ACT.Identity,
                               bias=bqk[:, g:g + 1]).then_inc(f_ready, 1)
                act.activation(qk_part[:, g, 0, :], ps[:, 2 + g, :], ACT.Identity,
                               bias=bqk[:, g:g + 1]).then_inc(f_ready, 1)

            move_xnT(0)
            act.wait_ge(w_in, 48)
            with act.Fori(0, NC - 1) as c:
                for g in range(4):
                    evacuate_qk(c, g)
                    if g == 1:
                        move_xnT(c + 1)
            for g in range(4):
                evacuate_qk(NC - 1, g)

            def copy_xnT(c, b):
                act.wait_ge(v_ready, c * 2 + (CREDIT[v_ready] - 2))
                act.activation(v_src[b], xnT[:, bass.ds(c, 1), :, :].rearrange("p a k t -> p (a k) t"),
                               ACT.Copy).then_inc(vsrc_ready, 1)

            def evacuate_v(c):
                for j in range(2):
                    act.wait_ge(v_ready, c * 2 + (j + 1 + CREDIT[v_ready]))
                    act.activation(v_rows[:, bass.ds(c * TPC + 2 * j, 2), :],
                                   ps[:, 4 + j, :].rearrange("p (a c) -> p a c", a=2), ACT.Copy).then_inc(v_evac, 1)

            copy_xnT(0, 0)
            with act.Fori(0, NC // 2 - 1) as c2:
                for b in range(2):
                    copy_xnT(c2 * 2 + (b + 1), 1 - b)
                    evacuate_v(c2 * 2 + b)
            copy_xnT(NC - 1, 1)
            evacuate_v(NC - 2)
            evacuate_v(NC - 1)

            def move_max_row(b, c, n):
                act.wait_ge(mrow_ready, n + 1 + CREDIT[mrow_ready])
                act.activation(q_stack[ROWS:ROWS + MROWS, b, bass.ds(c * CH, CH)], ps[0:MROWS, 7, :],
                               ACT.Copy).then_inc(mrow_done, 1)

            def exponential(g, i, it):
                if i == 0:
                    act.wait_ge(pv_done, it * KG + (g + 1))
                act.wait_ge(s_ready, it * (4 * KG) + (4 * g + i + 1))
                act.activation(probs[:, g % 4, i, :], ps[:, 4 + i % 2, :], ACT.Exp, scale=SCALE).then_inc(exp_done, 1)

            def move_aT(c):
                act.wait_ge(aT_psum, c + 1 + CREDIT[aT_psum])
                act.wait_ge(y_psum, c * 2 + CREDIT[y_psum])
                act.activation(aT, ps[:, 0:2, :], ACT.Copy).then_inc(aT_ready, 1)

            def attend(it, next_row, move_after={}):
                for g in range(KG):
                    for i in range(4):
                        if g in (8, KG - 1) and i == 2 and next_row:
                            odd = g // (KG - 1)
                            move_max_row(next_row[0], next_row[1] + odd, it * 2 + (2 + odd))
                        if g or i >= 2:
                            exponential(g, i, it)
                    if g in move_after:
                        move_aT(move_after[g])
                if next_row:
                    exponential(0, 0, it + 1)
                    exponential(0, 1, it + 1)
                act.wait_ge(pv_done, it * KG + (KG + CREDIT[pv_done]))
                act.wait_ge(comb_ready, it + 1)
                act.activation(o_sb[:, :], ps[:, 6, :], ACT.Copy).then_inc(o_evac, 1)

            move_max_row(0, 0, 0)
            move_max_row(0, 1, 1)
            exponential(0, 0, 0)
            exponential(0, 1, 0)
            with act.Fori(0, H // NB) as r:
                for b in range(NB):
                    first = r * (NB * PAIRS) + b * PAIRS
                    with act.Fori(0, PAIRS - 1) as j:
                        attend(first + j, (b, j * 2 + 2))
                    attend(first + (PAIRS - 1), ((b + 1) % NB, 0))
            with act.Fori(0, PAIRS - 1) as j:
                attend(j + (H - 1) * PAIRS, (0, j * 2 + 2))
            attend(ITS - 1, None, {5: 0, 12: 1})

            def move_wT(c, i):
                n = c * TPC + i
                act.wait_ge(wT_psum, n + 1 + CREDIT[wT_psum])
                act.wait_ge(agg_psum, n + CREDIT[agg_psum])
                act.activation(wT2, ps[:, 0:2, :], ACT.Copy).then_inc(wT_ready, 1)

            def exponentials(c, i):
                n = c * TPC + i
                act.wait_ge(picked_ready, n + 1)
                act.wait_ge(wT_psum, n - 1 + CREDIT[wT_psum])
                act.activation(wts[i % 2], ps[:, sc_bank[i % 2]:sc_bank[i % 2] + 2, :], ACT.Exp,
                               bias=nbias[:, i:i + 1], scale=RSQ).then_inc(e_ready, 1)

            def stage_block(c):
                act.wait_ge(h_ready, c + 1)
                act.wait_ge(hT_psum, c + CREDIT[hT_psum])
                act.activation(stage_h, v_rows[:, bass.ds(c * TPC, TPC), :], ACT.Copy).then_inc(stage_h_ready, 1)

            def ffn_chunk(c, two_ahead, one_ahead=True):
                act.wait_ge(hT_psum, c + 1 + CREDIT[hT_psum])
                act.activation(hT, ps[:, 0:2, :], ACT.Copy).then_inc(hT_ready, 1)
                act.wait_ge(qy_psum, c + 1)
                act.activation(queryT, ps[:, 4, :], ACT.Copy).then_inc(qy_ready, 1)
                act.wait_ge(rq_psum, c + 1)
                act.activation(rqT[0:RD, :], ps[0:RD, 6, :], ACT.Copy).then_inc(rq_ready, 1)
                act.wait_ge(u_psum, c + 1)
                act.activation(g1T[0:F1, :], ps[0:F1, 7, :], ACT.Gelu, bias=u1b[0:F1, :]).then_inc(u_ready, 1)
                exponentials(c, 0)
                if two_ahead:
                    move_aT(c + 2)
                move_wT(c, 0)
                for i in range(1, TPC):
                    exponentials(c, i)
                    move_wT(c, i)
                if one_ahead:
                    stage_block(c + 1)

            stage_block(0)
            with act.Fori(0, NC - 2) as c:
                ffn_chunk(c, True)
            ffn_chunk(NC - 2, False)
            ffn_chunk(NC - 1, False, False)
            act.activation(lv, hvar[:, :], ACT.Ln, bias=1.0).then_inc(lv_ready, 1)
            act.wait_ge(g_own, 3)
            act.activation(gtmp, learned, ACT.Exp, scale=-1.0).then_inc(g_e, 1)
            act.wait_ge(g_a, 1)
            act.activation(gtmp, gate, ACT.Exp, scale=-1.0).then_inc(g_e, 1)

            with act.Fori(0, NC // 4) as c4:
                for b in range(4):
                    act.wait_ge(o_rs, c4 * 4 + (b + 1))
                    for i in range(TPC):
                        last = act.activation(o2[b][:, i, :], o2[b][:, i, :], ACT.Identity,
                                              bias=o_shift[:, b, i:i + 1], scale=o_rstd[:, b, i:i + 1])
                    last.then_inc(z_ready, 1)

        @block.vector
        def _(dve):
            def tile_stats(src, n, own, mv_tiles=mv):
                dve.sem_inc(dve_passed, 1)
                for i in range(TPC):
                    last = dve.bn_stats(stats[:, i, :], src(i))
                last.then_inc(own, 1)
                dve.wait_ge(own, n + 1)
                dve.sem_inc(dve_passed, 1)
                for i in range(TPC):
                    last = dve.bn_aggr(mv_tiles[:, i, :], stats[:, i, :])
                return last

            def x_tile(c, i):
                return x_sb[:, bass.ds(c * TPC + i, 1), :].rearrange("p a c -> p (a c)")

            def x_stats(c):
                tile_stats(lambda i: x_tile(c, i), c, st_own).then_inc(st_done, 1)

            def norm_chunk(c):
                dve.wait_ge(rstd_done, c + 1)
                for i in range(TPC):
                    dve.tensor_scalar(xn[:, i, :], x_tile(c, i), mv[:, i, 0:1], rstd[:, i:i + 1],
                                      ALU.subtract, ALU.mult).then_inc(xn_ready, 1)

            def split(c, g):
                f, rest, part = qk_f32[:, g, :], qk_rest[:, g, :], qk_part[:, g, :, :]
                dve.wait_ge(f_ready, c * 8 + (2 * (g + 1) + CREDIT[f_ready]))
                dve.tensor_tensor(rest, f, part[:, 0, :], ALU.subtract).then_inc(split_own, 1)
                dve.wait_ge(split_own, c * 4 + (g + 1))
                dve.tensor_copy(part[:, 1, :], rest).then_inc(two_parts, 1)

            dve.wait_ge(x_in[0], 16)
            x_stats(0)
            dve.wait_ge(primed, 1)
            norm_chunk(0)
            dve.wait_ge(x_in[1], 16)
            x_stats(1)

            def x_chunk(c, stats_ahead):
                dve.wait_ge(t_ready, c + 1)
                norm_chunk(c + 1)
                split(c, 0)
                split(c, 1)
                if stats_ahead:
                    dve.wait_ge(x_in[2], 16 * (NC - 2))
                    x_stats(c + 2)
                split(c, 2)
                split(c, 3)

            with dve.Fori(0, NC - 2) as c:
                x_chunk(c, True)
            x_chunk(NC - 2, False)
            for g in range(4):
                split(NC - 1, g)

            def combine_used(it):
                o = ps[:, 7, 0:64 * TPC].rearrange("p (i e) -> p i e", i=TPC)[:, :, 0:2 * (D + 1)].rearrange(
                    "p i (a d) -> p i a d", a=2)
                dve.wait_ge(comb_ready, it + 1)
                dve.reciprocal(rinv[:, :, :], o[:, :, :, D]).then_inc(rinv_done, 1)
                dve.wait_ge(rinv_done, it + 1)
                dve.tensor_tensor(attn[:, bass.ds(it * (8 * D), 8 * D)].rearrange("p (a i d) -> p i a d", a=2, i=TPC),
                                  o[:, :, :, 0:D], rinv[:, :, :].unsqueeze(3).to_broadcast([P, TPC, 2, D]),
                                  ALU.mult).then_inc(comb_used, 1)

            def row_max(first, pieces, it):
                for p in pieces:
                    k, mi = p % 16, first + p // 16
                    if k == 0:
                        dve.wait_ge(negmax_ready, mi + CREDIT[negmax_ready])
                    dve.wait_ge(m_ready, mi * 16 + (k + 1))
                    dve.tensor_reduce(partial[:, k // 4, k % 4:k % 4 + 1], ps[:, 2 * (k % 2):2 * (k % 2) + 2, :], AX.XY,
                                      ALU.max).then_inc(max_used, 1)
                    if p == LEAD + 3 and it is not None:
                        combine_used(it)
                    if k == 15:
                        dve.wait_ge(max_used, mi * 16 + (16 + CREDIT[max_used]))
                        dve.wait_ge(nmparts_ready, mi + CREDIT[nmparts_ready])
                        dve.tensor_reduce(negmax[:, :], partial[:, :, :], AX.X, ALU.max,
                                          negate=True).then_inc(negmax_ready, 1)

            def h_tile(c, i):
                return v_rows[:, bass.ds(c * TPC + i, 1), :].rearrange("p a c -> p (a c)")

            def project_out(c):
                for j in range(2):
                    dve.wait_ge(y_psum, c * 2 + (j + 1 + CREDIT[y_psum]))
                    dve.tensor_tensor(v_rows[:, bass.ds(c * TPC + 2 * j, 2), :], ps[:, 2 + j, :].rearrange("p (a c) -> p a c", a=2),
                                      bproj, ALU.add).then_inc(y_evac, 1)

            def projected_stats(c):
                dve.wait_ge(y_evac, c * 2 + (2 + CREDIT[y_evac]))
                tile_stats(lambda i: h_tile(c, i), c * 7, y_own).then_inc(var_ready, 1)

            def add_block(c):
                dve.wait_ge(rs_ready, c * 2 + 1)
                for i in range(TPC):
                    last = dve.tensor_scalar(h_tile(c, i), h_tile(c, i), mv[:, i, 0:1], rstd[:, i:i + 1],
                                             ALU.subtract, ALU.mult)
                last.then_inc(y_own, 1)
                dve.wait_ge(y_own, c * 7 + 2)
                xc = x_sb[:, bass.ds(c * TPC, TPC), :]
                dve.tensor_tensor(xc, xc, v_rows[:, bass.ds(c * TPC, TPC), :], ALU.add).then_inc(y_own, 1)

            def block_stats(c):
                dve.wait_ge(y_own, c * 7 + 3)
                tile_stats(lambda i: x_tile(c, i), c * 7 + 3, y_own).then_inc(var_ready, 1)

            def norm_block(c):
                dve.wait_ge(rs_ready, c * 2 + 2)
                for i in range(TPC):
                    last = dve.tensor_scalar(h_tile(c, i), x_tile(c, i), mv[:, i, 0:1], rstd[:, i:i + 1],
                                             ALU.subtract, ALU.mult)
                last.then_inc(h_ready, 1)

            def norm_stats(c):
                dve.wait_ge(h_ready, c + 1)
                tile_stats(lambda i: h_tile(c, i), c * 7 + 4, y_own).then_inc(y_own, 1)
                dve.wait_ge(y_own, c * 7 + 6)
                dve.tensor_copy(hvar[:, bass.ds(c * TPC, TPC)], mv[:, 0:TPC, 1]).then_inc(y_own, 1)
                dve.wait_ge(y_own, c * 7 + 7)

            def take_top(c, i):
                n = c * TPC + i
                sc = ps[:, sc_bank[i % 2]:sc_bank[i % 2] + 2, :]
                dve.wait_ge(sc_psum, n + 1)
                dve.sem_inc(dve_passed, 1)
                dve.max(top8[:, i, :], sc).then_inc(top_ready, 1)
                dve.wait_ge(top_ready, n + 1)
                dve.tensor_scalar(nbias[:, i:i + 1], top8[:, i, 0:1], -RSQ, None, ALU.mult)
                dve.match_replace(picked[i % 2], top8[:, i, :], sc, TAKEN).then_inc(picked_ready, 1)

            def weigh(c, i):
                n = c * TPC + i
                dve.wait_ge(e_ready, n + 1 + CREDIT[e_ready])
                dve.wait_ge(picked_ready, n + 1)
                dve.scalar_tensor_tensor(out=wts_flat[i % 2], in0=picked_flat[i % 2], scalar=TAKEN, in1=wts_flat[i % 2],
                                         op0=ALU.is_equal, op1=ALU.mult,
                                         accum_out=wsum[:, i:i + 1]).then_inc(w_sum, 1)
                dve.wait_ge(w_sum, n + 1)
                dve.reciprocal(wrec[:, i:i + 1], wsum[:, i:i + 1]).then_inc(wr_ready, 1)

            def keep_agg(c, i):
                n = c * TPC + i
                dve.wait_ge(agg_psum, n + 1 + CREDIT[agg_psum])
                dve.wait_ge(wr_ready, n + 1)
                dve.tensor_scalar(agg_tile(n), ps[:, 2 + i % 2, 0:C].rearrange("p (h d) -> p h d", h=H),
                                  wrec[:, i:i + 1], None, ALU.mult).then_inc(agg_ready, 1)

            def ffn_chunk(c, ahead):
                take_top(c, 0)
                if ahead:
                    project_out(c + 1)
                weigh(c, 0)
                dve.wait_ge(l_psum, c + 1)
                dve.tensor_copy(learned[:, bass.ds(c * TPC, TPC)], ps[:, 3, 0:TPC]).then_inc(l_ready, 1)
                take_top(c, 1)
                if ahead:
                    projected_stats(c + 1)
                weigh(c, 1)
                take_top(c, 2)
                keep_agg(c, 0)
                if ahead:
                    add_block(c + 1)
                weigh(c, 2)
                take_top(c, 3)
                keep_agg(c, 1)
                if ahead:
                    block_stats(c + 1)
                weigh(c, 3)
                if ahead:
                    norm_block(c + 1)
                keep_agg(c, 2)
                if ahead:
                    norm_stats(c + 1)
                keep_agg(c, 3)

            with dve.Fori(0, AHEAD) as c:
                row_max(c, range(16), None)
            row_max(AHEAD, range(LEAD), None)
            with dve.Fori(0, ITS - 2) as it:
                row_max(it * 2 + AHEAD, range(LEAD, LEAD + 32), it)
            row_max((ITS - 2) * 2 + AHEAD, range(LEAD, 32), ITS - 2)
            combine_used(ITS - 1)
            for n, (dst, src) in enumerate((
                (keysT.rearrange("p (a n) -> p a n", a=2), ps[:, 0:2, :]),
                (qpT, ps[:, 2, 0:2 * P].rearrange("p (k n) -> p k n", k=CC)),
                (routT, ps[:, 2, 2 * P:2 * P + RD]),
                (u1T, ps[:, 2, 3 * P:4 * P].rearrange("p (k n) -> p k n", k=CC)),
            )):
                if n == 0:
                    dve.wait_ge(w3_t, 1)
                dve.tensor_copy(dst, src).then_inc(w3_e, 1)
            dve.tensor_scalar(rkT[MASKROW:MASKROW + 1, :], rkT[MASKROW:MASKROW + 1, :], float(RD) ** 0.5, None,
                              ALU.mult).then_inc(w3_e, 1)
            dve.wait_ge(w3_t, 2)
            dve.tensor_copy(rkT[0:RD, :].rearrange("p (a n) -> p a n", a=2), ps[0:RD, 0:2, :]).then_inc(w3_e, 1)
            project_out(0)
            projected_stats(0)
            add_block(0)
            block_stats(0)
            norm_block(0)
            norm_stats(0)
            combine_used(ITS)
            with dve.Fori(0, NC - 1) as c:
                ffn_chunk(c, True)
            ffn_chunk(NC - 1, False)

            def step(sem_, n, ins):
                ins.then_inc(sem_, 1)
                dve.wait_ge(sem_, n)

            dve.wait_ge(lv_ready, 1)
            dve.reduce_sum(lvs, lv, axis=AX.X).then_inc(lv_own, 1)
            dve.tensor_scalar(learned, learned, u2b, None, ALU.add).then_inc(g_own, 1)
            dve.wait_ge(lvt_ready, 1)
            dve.tensor_scalar(lvm, ps[:, 2, 0:1], 1.0 / T, 1e-6, ALU.mult, ALU.add).then_inc(g_own, 1)
            dve.wait_ge(g_own, 2)
            dve.reciprocal(lvr, lvm).then_inc(g_own, 1)
            dve.wait_ge(g_own, 3)
            dve.tensor_scalar(lv, lv, lvr, 0.5, ALU.mult, ALU.mult).then_inc(g_own, 1)
            dve.wait_ge(g_e, 1)
            dve.tensor_scalar(gtmp, gtmp, 1.0, None, ALU.add).then_inc(g_own, 1)
            dve.wait_ge(g_own, 5)
            dve.reciprocal(gate, gtmp).then_inc(g_own, 1)
            dve.wait_ge(g_own, 6)
            dve.scalar_tensor_tensor(out=lv, in0=gate, scalar=2.5, in1=lv, op0=ALU.mult, op1=ALU.add).then_inc(g_own, 1)
            dve.wait_ge(g_own, 7)
            dve.tensor_scalar(lv, lv, 0.0, 5.0, ALU.max, ALU.min).then_inc(g_own, 1)
            dve.wait_ge(g_own, 8)
            dve.tensor_scalar(gate, lv, gw, gb, ALU.mult, ALU.add).then_inc(g_a, 1)
            dve.wait_ge(g_e, 2)
            dve.tensor_scalar(gtmp, gtmp, 1.0, None, ALU.add).then_inc(g_own, 1)
            dve.wait_ge(g_own, 9)
            dve.reciprocal(gate, gtmp).then_inc(g_own, 1)
            dve.wait_ge(g_own, 10)

            with dve.Fori(0, NC // 4) as c4:
                for b in range(4):
                    c = c4 * 4 + b
                    own = c4 * 12 + 3 * b
                    dve.wait_ge(res_ready, c4 * 4 + (b - 3 + CREDIT[res_ready]))
                    for i in range(TPC):
                        n = c * TPC + i
                        last = dve.scalar_tensor_tensor(
                            out=o2[b][:, i, :].rearrange("p (h d) -> p h d", h=H), in0=agg_tile(n),
                            scalar=gate[:, bass.ds(n, 1)], in1=h_tile(c, i).rearrange("p (h d) -> p h d", h=H),
                            op0=ALU.mult, op1=ALU.add)
                    last.then_inc(o_own, 1)
                    dve.wait_ge(o_own, own + 1)
                    tile_stats(lambda i: o2[b][:, i, :], own + 1, o_own, o_mv[:, b, :, :]).then_inc(o_own, 1)
                    dve.wait_ge(o_own, own + 3)
                    dve.tensor_scalar(o_nmean[:, b, :], o_mv[:, b, :, 0], -1.0, None, ALU.mult).then_inc(o_var, 1)

        @block.tensor
        def _(pe):
            def transpose_chunk(src, done):
                for i in range(TPC):
                    for k in range(CC):
                        last = pe.transpose(ps[:, k, P * i:P * (i + 1)], src[:, i, P * k:P * (k + 1)], ident[:, :])
                last.then_inc(done, 1)

            def project_qk(c, g):
                if g == 0:
                    pe.wait_ge(xnT_ready, c + 1)
                pe.wait_ge(f_ready, c * 8 + 2 * (g + 1))
                for k in range(CC):
                    last = pe.matmul(ps[:, 2 + g, :], wqkv[:, k, P * g:P * (g + 1)], xnT_block(c, k),
                                     start=(k == 0), stop=(k == CC - 1))
                last.then_inc(qk_ready, 1)

            def xnT_block(c, k):
                return xnT[:, bass.ds(c, 1), k, :].rearrange("p a t -> p (a t)")

            def project_v(c, b, j):
                pe.wait_ge(vsrc_ready, c + 1)
                pe.wait_ge(v_evac, c * 2 + (j + 1))
                for a in range(2):
                    i = 2 * j + a
                    for k in range(CC):
                        last = pe.matmul(ps[:, 4 + j, C * a:C * (a + 1)], v_src[b][:, k, P * i:P * (i + 1)],
                                         wqkv[:, k, 2 * C:3 * C], start=(k == 0), stop=(k == CC - 1))
                last.then_inc(v_ready, 1)

            pe.wait_ge(primed, 1)
            pe.wait_ge(xn_ready, TPC)
            transpose_chunk(xn, t_ready)
            pe.wait_ge(wqkv_in, 16)
            with pe.Fori(0, NC - 1) as c:
                project_qk(c, 0)
                project_qk(c, 1)
                pe.wait_ge(xn_ready, c * TPC + 2 * TPC)
                transpose_chunk(xn, t_ready)
                project_qk(c, 2)
                project_qk(c, 3)
            for g in range(4):
                project_qk(NC - 1, g)
            with pe.Fori(0, NC // 4) as c2:
                for b in range(2):
                    for j in range(2):
                        project_v(c2 * 2 + b, b, j)

            def max_pair(k, mi, b1, c):
                pe.wait_ge(max_used, mi * 16 + (k + 1))
                for e in range(2):
                    last = pe.matmul(ps[:, 2 * (k % 2) + e, :], q_stack[0:ROWS, b1, bass.ds(c * CH + (k // 4) * P, P)],
                                     k_stack[0:ROWS, b1, CH * (2 * (k % 4) + e):CH * (2 * (k % 4) + e + 1)],
                                     start=True, stop=True)
                last.then_inc(m_ready, 1)

            def score(g, i, it, b, j):
                pe.wait_ge(exp_done, it * (4 * KG) + (4 * g + i + 1))
                tile = 2 * g + i % 2
                pe.matmul(ps[:, 4 + i % 2, :], k_stack[0:ROWS + MROWS, b, P * tile:P * (tile + 1)],
                          q_stack[0:ROWS + MROWS, b, bass.ds(j * (2 * CH) + (i // 2) * CH, CH)],
                          start=True, stop=True).then_inc(s_ready, 1)

            def weighted_values(g, it, b):
                pe.wait_ge(exp_done, it * (4 * KG) + (4 * g + 4 + CREDIT[exp_done]))
                if g == 0:
                    pe.wait_ge(o_evac, it + 1)
                for i in range(4):
                    last = pe.matmul(ps[32 * i:32 * i + 32, 6, :], v_head[:, b, 2 * g + i % 2, :], probs[:, g % 4, i, :],
                                     start=(g == 0), stop=(g == KG - 1))
                last.then_inc(pv_done, 1)

            def combine(it):
                pe.wait_ge(o_evac, it + 1)
                pe.wait_ge(comb_used, it + 1)
                for i in range(TPC):
                    last = pe.matmul(ps[:, 7, 64 * i:64 * i + 2 * (D + 1)], o_sb[:, P * i:P * (i + 1)], sel[:, :],
                                     start=True, stop=True)
                last.then_inc(comb_ready, 1)

            def max_row(n, combined):
                pe.wait_ge(nmparts_ready, n + 1 + CREDIT[nmparts_ready])
                pe.wait_ge(mrow_done, n + CREDIT[mrow_done])
                pe.wait_ge(comb_used, combined + CREDIT[comb_used])
                for i in range(TPC):
                    last = pe.matmul(ps[0:MROWS, 7, P * i:P * (i + 1)], nm_parts[:, i, :], ident_bf[:, :],
                                     start=True, stop=True)
                last.then_inc(mrow_ready, 1)

            def first_scores(it, b, j):
                pe.wait_ge(mrow_done, it * 2 + (1 + CREDIT[mrow_done]))
                score(0, 0, it, b, j)
                score(0, 1, it, b, j)

            def attend(it, b, j, ahead, following, extra={}):
                for g in range(KG):
                    if g:
                        score(g, 0, it, b, j)
                        score(g, 1, it, b, j)
                        weighted_values(g - 1, it, b)
                    else:
                        pe.wait_ge(mrow_done, it * 2 + (2 + CREDIT[mrow_done]))
                    score(g, 2, it, b, j)
                    score(g, 3, it, b, j)
                    for p in (LEAD + 2 * g, LEAD + 2 * g + 1):
                        if p // 16 < len(ahead):
                            max_pair(p % 16, it * 2 + (AHEAD + p // 16), *ahead[p // 16])
                    if g == 1:
                        combine(it)
                    if g in (7, KG - 2) and following:
                        max_row(it * 2 + (AHEAD + g // (KG - 2)), it + 1)
                    if g in extra:
                        extra[g]()
                if following:
                    first_scores(it + 1, *following)
                weighted_values(KG - 1, it, b)

            pe.wait_ge(stack_in[0], 16 * 12)
            with pe.Fori(0, AHEAD) as c:
                for k in range(16):
                    max_pair(k, c, 0, c)
                    if k % 4 == 1:
                        project_v(c * 2 + (NC // 2 + k // 8), k // 8, k // 4 % 2)
            max_row(0, 0)
            for k in range(LEAD):
                max_pair(k, AHEAD, 0, AHEAD)
            max_row(1, 0)
            pe.wait_ge(vhead_ready, 1)
            first_scores(0, 0, 0)
            with pe.Fori(0, H // NB) as r:
                for b in range(NB):
                    first = r * (NB * PAIRS) + b * PAIRS
                    b1 = (b + 1) % NB
                    pe.wait_ge(vhead_ready, r * NB + (b + 1))
                    pe.sem_inc(pe_passed, 1)
                    with pe.Fori(0, PAIRS - 2) as j:
                        attend(first + j, b, j, [(b, j * 2 + c) for c in (2, 3, 4)], (b, j + 1))
                    pe.wait_ge(stack_in[b1], (r + 1 + (b + 1) // NB) * (16 * 12))
                    attend(first + (PAIRS - 2), b, PAIRS - 2, [(b, NC - 2), (b, NC - 1), (b1, 0)], (b, PAIRS - 1))
                    attend(first + (PAIRS - 1), b, PAIRS - 1, [(b1, 0), (b1, 1), (b1, 2)], (b1, 0))
            def transpose_weights():
                pe.wait_ge(w3_in, 16 * W3_LOADS)
                pe.wait_ge(max_used, H * NC * 16 + CREDIT[max_used])
                for v in range(NV):
                    pe.transpose(ps[:, v // 4, P * (v % 4):P * (v % 4 + 1)], keys[:, v, :], ident[:, :])
                for k in range(CC):
                    pe.transpose(ps[:, 2, P * k:P * (k + 1)], qpw[:, P * k:P * (k + 1)], ident[:, :])
                    pe.transpose(ps[:, 2, 3 * P + F1 * k:3 * P + F1 * (k + 1)], u1w[0:F1, P * k:P * (k + 1)],
                                 ident[0:F1, 0:F1])
                pe.transpose(ps[:, 2, 2 * P:2 * P + RD], routw[0:RD, :], ident[0:RD, 0:RD]).then_inc(w3_t, 1)

            def route_keys():
                pe.wait_ge(w3_e, 4)
                for a in range(2):
                    last = pe.matmul(ps[0:RD, a, :], routT, keysT[:, CH * a:CH * (a + 1)], start=True, stop=True)
                last.then_inc(w3_t, 1)

            def attn_transpose(c):
                pe.wait_ge(stage_a_ready, c + 1)
                transpose_chunk(stage_a, aT_psum)

            def project_out(c, j):
                pe.wait_ge(aT_ready, c + 1)
                pe.wait_ge(y_evac, c * 2 + (j + 1))
                for a in range(2):
                    i = 2 * j + a
                    for k in range(CC):
                        last = pe.matmul(ps[:, 2 + j, C * a:C * (a + 1)], aT[:, k, P * i:P * (i + 1)], wproj[:, k, :],
                                         start=(k == 0), stop=(k == CC - 1))
                last.then_inc(y_psum, 1)

            def first_transpose():
                pe.wait_ge(w3_e, 6)
                attn_transpose(0)

            first = (H - 1) * PAIRS
            pe.wait_ge(vhead_ready, H)
            with pe.Fori(0, PAIRS - 2) as j:
                attend(j + first, 0, j, [(0, j * 2 + c) for c in (2, 3, 4)], (0, j + 1))
            attend(ITS - 2, 0, PAIRS - 2, [(0, NC - 2), (0, NC - 1)], (0, PAIRS - 1))
            attend(ITS - 1, 0, PAIRS - 1, [], None,
                   {1: transpose_weights, 3: route_keys, 5: first_transpose, 7: lambda: project_out(0, 0),
                    8: lambda: project_out(0, 1), 12: lambda: attn_transpose(1)})
            combine(ITS)


            def lookup_scores(c, i):
                n = c * TPC + i
                pe.wait_ge(e_ready, n - 1 + CREDIT[e_ready])
                for a in range(2):
                    last = pe.matmul(ps[:, sc_bank[i % 2] + a, :], rqT[0:MASKROW + 1, P * i:P * (i + 1)],
                                     rkT[0:MASKROW + 1, CH * a:CH * (a + 1)], start=True, stop=True)
                last.then_inc(sc_psum, 1)

            def ffn_chunk(c, one_ahead, two_ahead):
                pe.wait_ge(wT_ready, c * TPC + CREDIT[wT_ready])
                pe.wait_ge(stage_h_ready, c + 1)
                transpose_chunk(stage_h, hT_psum)
                pe.wait_ge(agg_ready, c * TPC + CREDIT[agg_ready])
                if one_ahead:
                    project_out(c + 1, 0)
                pe.wait_ge(hT_ready, c + 1)
                pe.wait_ge(e_ready, c * TPC + CREDIT[e_ready])
                for k in range(CC):
                    last = pe.matmul(ps[:, 4, :], qpT[:, k, :], hT[:, k, :], start=(k == 0), stop=(k == CC - 1))
                last.then_inc(qy_psum, 1)
                for k in range(CC):
                    last = pe.matmul(ps[0:F1, 7, :], u1T[:, k, :], hT[:, k, :], start=(k == 0), stop=(k == CC - 1))
                last.then_inc(u_psum, 1)
                pe.wait_ge(qy_ready, c + 1)
                pe.matmul(ps[0:RD, 6, :], routT, queryT, start=True, stop=True).then_inc(rq_psum, 1)
                pe.wait_ge(rq_ready, c + 1)
                lookup_scores(c, 0)
                if one_ahead:
                    project_out(c + 1, 1)
                pe.wait_ge(u_ready, c + 1)
                lookup_scores(c, 1)
                if one_ahead:
                    pe.wait_ge(y_evac, c * 2 + (4 + CREDIT[y_evac]))
                for i in range(TPC):
                    last = pe.matmul(ps[:, 3, i:i + 1], g1T[0:F1, P * i:P * (i + 1)], u2w[0:F1, :], start=True, stop=True)
                last.then_inc(l_psum, 1)
                if two_ahead:
                    attn_transpose(c + 2)
                    pe.wait_ge(aT_ready, c + 3)
                for i in range(TPC):
                    n = c * TPC + i
                    pe.wait_ge(wr_ready, n + 1)
                    pe.wait_ge(wT_ready, n + CREDIT[wT_ready])
                    for v in range(NV):
                        last = pe.transpose(ps[:, v // 4, P * (v % 4):P * (v % 4 + 1)],
                                            wts_flat[i % 2][:, P * v:P * (v + 1)], ident[:, :])
                    last.then_inc(wT_psum, 1)
                    if i + 2 < TPC:
                        lookup_scores(c, i + 2)
                    pe.wait_ge(wT_ready, n + 1 + CREDIT[wT_ready])
                    if i == 1:
                        pe.wait_ge(l_ready, c + 1 + CREDIT[l_ready])
                    if i >= 2:
                        pe.wait_ge(agg_ready, n - 1 + CREDIT[agg_ready])
                    for v in range(NV):
                        last = pe.matmul(ps[:, 2 + i % 2, 0:C], wT[:, v, :], values[:, v, :],
                                         start=(v == 0), stop=(v == NV - 1))
                    last.then_inc(agg_psum, 1)

            pe.wait_ge(aT_ready, 2)
            pe.wait_ge(w3_init, 4)
            with pe.Fori(0, NC - 2) as c:
                ffn_chunk(c, True, True)
            ffn_chunk(NC - 2, True, False)
            ffn_chunk(NC - 1, False, False)
            pe.wait_ge(lv_own, 1)
            pe.wait_ge(agg_ready, NT + CREDIT[agg_ready])
            pe.matmul(ps[:, 2, 0:1], ones, lvs, start=True, stop=True).then_inc(lvt_ready, 1)


INPUTS = ["L0_attn_x", "L0_attn_w_qkv", "L0_attn_b_qkv", "L0_attn_w_proj", "L0_attn_b_proj", "L0_ffn_q_proj_w",
          "L0_ffn_router_w", "L0_ffn_aux_keys", "L0_ffn_aux_values", "L0_ffn_reliability_mask", "L0_ffn_unc_w1",
          "L0_ffn_unc_b1", "L0_ffn_unc_w2", "L0_ffn_unc_b2", "L0_ffn_gate_w1", "L0_ffn_gate_bias"]


def kernel(**inputs):
    import numpy as np
    import concourse.bacc as bacc
    from concourse.bass_utils import run_bass_kernel_spmd

    nc = bacc.Bacc("TRN2", target_bir_lowering=False, num_devices=1)
    arrays, args = {}, []
    for name in INPUTS:
        a = np.ascontiguousarray(inputs[name])
        arrays[name] = a
        args.append(nc.dram_tensor(name, a.shape, mybir.dt.from_np(a.dtype), kind="ExternalInput").ap())
    shape = arrays["L0_attn_x"].shape
    args.append(nc.dram_tensor("out", shape, F32, kind="ExternalOutput").ap())
    sandwich_kernel(nc, *args)
    result = run_bass_kernel_spmd(nc, [arrays], core_ids=[0])
    return result.results[0]["out"]
```
